# Optimizing a Trainium2 kernel written in Bass

```python
import numpy as np
import jax
import jax.numpy as jnp

def _softmax(x, axis=-1):
    return jax.nn.softmax(x, axis=axis)

def _gelu(x):
    return jax.nn.gelu(x, approximate=True)

def _silu(x):
    return jax.nn.silu(x)

def _sigmoid(x):
    return jax.nn.sigmoid(x)

def _layernorm(x, axis=-1, eps=1e-05):
    m = jnp.mean(x, axis=axis, keepdims=True)
    v = jnp.var(x, axis=axis, keepdims=True)
    return (x - m) / jnp.sqrt(v + eps)

def _scatter_add(tgt, idx, src, axis=0):
    return tgt.at[idx].add(src)

def _segment_sum(src, seg, n):
    return jax.ops.segment_sum(src, seg, n)
kernel_name = 'mk_dlrm_tower_d1_rec_r8_5dce54'

def setup_inputs(seed: int=0):
    np.random.seed(seed)
    _w = jnp.asarray

    def _rec_inputs():
        import jax
        import jax.numpy as jnp
        _tk = jax.random.key(seed)
        dense_ctx = jax.random.normal(jax.random.fold_in(_tk, 190), (2048, 16), jnp.float32)
        ids = jnp.stack([jax.random.randint(jax.random.fold_in(_tk, 200 + f), (2048,), 0, v, jnp.int32) for f, v in enumerate([1250, 1000, 1000, 1000, 12500, 1250, 1250, 1000, 12500, 1000, 1250, 1000, 12500, 1000, 1000, 1000, 12500, 12500, 1250, 1000, 1000, 1000, 12500, 1250, 1250, 1000, 1000, 12500, 1000, 12500, 1000, 1000])], axis=1)
        tbl_0 = 0.05 * jax.random.normal(jax.random.fold_in(_tk, 500 + 0), (1250, 256), jnp.float32)
        tbl_1 = 0.05 * jax.random.normal(jax.random.fold_in(_tk, 500 + 1), (1000, 256), jnp.float32)
        tbl_2 = 0.05 * jax.random.normal(jax.random.fold_in(_tk, 500 + 2), (1000, 256), jnp.float32)
        tbl_3 = 0.05 * jax.random.normal(jax.random.fold_in(_tk, 500 + 3), (1000, 256), jnp.float32)
        tbl_4 = 0.05 * jax.random.normal(jax.random.fold_in(_tk, 500 + 4), (12500, 256), jnp.float32)
        tbl_5 = 0.05 * jax.random.normal(jax.random.fold_in(_tk, 500 + 5), (1250, 256), jnp.float32)
        tbl_6 = 0.05 * jax.random.normal(jax.random.fold_in(_tk, 500 + 6), (1250, 256), jnp.float32)
        tbl_7 = 0.05 * jax.random.normal(jax.random.fold_in(_tk, 500 + 7), (1000, 256), jnp.float32)
        tbl_8 = 0.05 * jax.random.normal(jax.random.fold_in(_tk, 500 + 8), (12500, 256), jnp.float32)
        tbl_9 = 0.05 * jax.random.normal(jax.random.fold_in(_tk, 500 + 9), (1000, 256), jnp.float32)
        tbl_10 = 0.05 * jax.random.normal(jax.random.fold_in(_tk, 500 + 10), (1250, 256), jnp.float32)
        tbl_11 = 0.05 * jax.random.normal(jax.random.fold_in(_tk, 500 + 11), (1000, 256), jnp.float32)
        tbl_12 = 0.05 * jax.random.normal(jax.random.fold_in(_tk, 500 + 12), (12500, 256), jnp.float32)
        tbl_13 = 0.05 * jax.random.normal(jax.random.fold_in(_tk, 500 + 13), (1000, 256), jnp.float32)
        tbl_14 = 0.05 * jax.random.normal(jax.random.fold_in(_tk, 500 + 14), (1000, 256), jnp.float32)
        tbl_15 = 0.05 * jax.random.normal(jax.random.fold_in(_tk, 500 + 15), (1000, 256), jnp.float32)
        tbl_16 = 0.05 * jax.random.normal(jax.random.fold_in(_tk, 500 + 16), (12500, 256), jnp.float32)
        tbl_17 = 0.05 * jax.random.normal(jax.random.fold_in(_tk, 500 + 17), (12500, 256), jnp.float32)
        tbl_18 = 0.05 * jax.random.normal(jax.random.fold_in(_tk, 500 + 18), (1250, 256), jnp.float32)
        tbl_19 = 0.05 * jax.random.normal(jax.random.fold_in(_tk, 500 + 19), (1000, 256), jnp.float32)
        tbl_20 = 0.05 * jax.random.normal(jax.random.fold_in(_tk, 500 + 20), (1000, 256), jnp.float32)
        tbl_21 = 0.05 * jax.random.normal(jax.random.fold_in(_tk, 500 + 21), (1000, 256), jnp.float32)
        tbl_22 = 0.05 * jax.random.normal(jax.random.fold_in(_tk, 500 + 22), (12500, 256), jnp.float32)
        tbl_23 = 0.05 * jax.random.normal(jax.random.fold_in(_tk, 500 + 23), (1250, 256), jnp.float32)
        tbl_24 = 0.05 * jax.random.normal(jax.random.fold_in(_tk, 500 + 24), (1250, 256), jnp.float32)
        tbl_25 = 0.05 * jax.random.normal(jax.random.fold_in(_tk, 500 + 25), (1000, 256), jnp.float32)
        tbl_26 = 0.05 * jax.random.normal(jax.random.fold_in(_tk, 500 + 26), (1000, 256), jnp.float32)
        tbl_27 = 0.05 * jax.random.normal(jax.random.fold_in(_tk, 500 + 27), (12500, 256), jnp.float32)
        tbl_28 = 0.05 * jax.random.normal(jax.random.fold_in(_tk, 500 + 28), (1000, 256), jnp.float32)
        tbl_29 = 0.05 * jax.random.normal(jax.random.fold_in(_tk, 500 + 29), (12500, 256), jnp.float32)
        tbl_30 = 0.05 * jax.random.normal(jax.random.fold_in(_tk, 500 + 30), (1000, 256), jnp.float32)
        tbl_31 = 0.05 * jax.random.normal(jax.random.fold_in(_tk, 500 + 31), (1000, 256), jnp.float32)
        _rk = jax.random.fold_in(_tk, 7)
        W_top1 = 0.0441942 * jax.random.normal(jax.random.fold_in(_tk, 801), (512, 512), jnp.float32)
        W_top2 = 0.0441942 * jax.random.normal(jax.random.fold_in(_tk, 802), (512, 256), jnp.float32)
        W_top3 = 0.0625 * jax.random.normal(jax.random.fold_in(_tk, 803), (256, 1), jnp.float32)
        b_top1 = jnp.zeros((512,), jnp.float32)
        b_top2 = jnp.zeros((256,), jnp.float32)
        return (dense_ctx, ids, tbl_0, tbl_1, tbl_2, tbl_3, tbl_4, tbl_5, tbl_6, tbl_7, tbl_8, tbl_9, tbl_10, tbl_11, tbl_12, tbl_13, tbl_14, tbl_15, tbl_16, tbl_17, tbl_18, tbl_19, tbl_20, tbl_21, tbl_22, tbl_23, tbl_24, tbl_25, tbl_26, tbl_27, tbl_28, tbl_29, tbl_30, tbl_31, W_top1, b_top1, W_top2, b_top2, W_top3)
    dense_ctx, ids, tbl_0, tbl_1, tbl_2, tbl_3, tbl_4, tbl_5, tbl_6, tbl_7, tbl_8, tbl_9, tbl_10, tbl_11, tbl_12, tbl_13, tbl_14, tbl_15, tbl_16, tbl_17, tbl_18, tbl_19, tbl_20, tbl_21, tbl_22, tbl_23, tbl_24, tbl_25, tbl_26, tbl_27, tbl_28, tbl_29, tbl_30, tbl_31, W_top1, b_top1, W_top2, b_top2, W_top3 = _rec_inputs()

    def _L0_rec_setup():
        import jax, jax.numpy as jnp
        import numpy as np
        B, N, D = (1024, 32, 256)
        key = jax.random.key(seed)
        x = jax.random.normal(key, (B, N, D), dtype=jnp.float32)
        return {'x': x}
    _L0_rec_all = _L0_rec_setup()
    _L0_rec_in = {k: v for k, v in _L0_rec_all.items() if k in ()}
    del _L0_rec_all
    return {'dense_ctx': dense_ctx, 'ids': ids, 'tbl_0': tbl_0, 'tbl_1': tbl_1, 'tbl_2': tbl_2, 'tbl_3': tbl_3, 'tbl_4': tbl_4, 'tbl_5': tbl_5, 'tbl_6': tbl_6, 'tbl_7': tbl_7, 'tbl_8': tbl_8, 'tbl_9': tbl_9, 'tbl_10': tbl_10, 'tbl_11': tbl_11, 'tbl_12': tbl_12, 'tbl_13': tbl_13, 'tbl_14': tbl_14, 'tbl_15': tbl_15, 'tbl_16': tbl_16, 'tbl_17': tbl_17, 'tbl_18': tbl_18, 'tbl_19': tbl_19, 'tbl_20': tbl_20, 'tbl_21': tbl_21, 'tbl_22': tbl_22, 'tbl_23': tbl_23, 'tbl_24': tbl_24, 'tbl_25': tbl_25, 'tbl_26': tbl_26, 'tbl_27': tbl_27, 'tbl_28': tbl_28, 'tbl_29': tbl_29, 'tbl_30': tbl_30, 'tbl_31': tbl_31, 'W_top1': W_top1, 'b_top1': b_top1, 'W_top2': W_top2, 'b_top2': b_top2, 'W_top3': W_top3}

def reference(dense_ctx, ids, tbl_0, tbl_1, tbl_2, tbl_3, tbl_4, tbl_5, tbl_6, tbl_7, tbl_8, tbl_9, tbl_10, tbl_11, tbl_12, tbl_13, tbl_14, tbl_15, tbl_16, tbl_17, tbl_18, tbl_19, tbl_20, tbl_21, tbl_22, tbl_23, tbl_24, tbl_25, tbl_26, tbl_27, tbl_28, tbl_29, tbl_30, tbl_31, W_top1, b_top1, W_top2, b_top2, W_top3):
    import jax
    import jax.numpy as jnp

    def _L0_rec_ref(x):
        import jax, jax.numpy as jnp
        import numpy as np
        B, N, D = (1024, 32, 256)
        'Second-order feature interaction (DLRM dot interaction).\n\n            Computes dot(x_i, x_j) for all field pairs i < j (self_interaction=False),\n            flattened in row-major upper-triangular order -> [B, N*(N-1)/2].\n            Matches tf.boolean_mask(dot_products, strictly_upper_mask) ordering.\n            '
        b, n, d = x.shape
        iu, ju = jnp.triu_indices(n, k=1)
        dots = jnp.einsum('bnd,bmd->bnm', x, x)
        return dots[:, iu, ju]
    e = jnp.stack([tbl_0[ids[:, 0]], tbl_1[ids[:, 1]], tbl_2[ids[:, 2]], tbl_3[ids[:, 3]], tbl_4[ids[:, 4]], tbl_5[ids[:, 5]], tbl_6[ids[:, 6]], tbl_7[ids[:, 7]], tbl_8[ids[:, 8]], tbl_9[ids[:, 9]], tbl_10[ids[:, 10]], tbl_11[ids[:, 11]], tbl_12[ids[:, 12]], tbl_13[ids[:, 13]], tbl_14[ids[:, 14]], tbl_15[ids[:, 15]], tbl_16[ids[:, 16]], tbl_17[ids[:, 17]], tbl_18[ids[:, 18]], tbl_19[ids[:, 19]], tbl_20[ids[:, 20]], tbl_21[ids[:, 21]], tbl_22[ids[:, 22]], tbl_23[ids[:, 23]], tbl_24[ids[:, 24]], tbl_25[ids[:, 25]], tbl_26[ids[:, 26]], tbl_27[ids[:, 27]], tbl_28[ids[:, 28]], tbl_29[ids[:, 29]], tbl_30[ids[:, 30]], tbl_31[ids[:, 31]]], axis=1)
    z = _L0_rec_ref(e)
    z = z.reshape(z.shape[0], -1)
    h = jnp.concatenate([z, dense_ctx], axis=1)
    h = jnp.maximum(h @ W_top1 + b_top1, 0.0)
    h = jnp.maximum(h @ W_top2 + b_top2, 0.0)
    y = h @ W_top3
    return y

_drawn_inputs = setup_inputs


def setup_inputs(seed=0):
    import zlib

    import numpy as np

    out = dict(_drawn_inputs(seed))
    spreads = {'b_top1': (0.0, 0.1), 'b_top2': (0.0, 0.1)}
    factors = {}
    for name, (base, spread) in spreads.items():
        noise = np.random.default_rng([zlib.crc32(name.encode()), seed]).standard_normal(out[name].shape)
        drawn = base * np.exp(spread * noise) if base else spread * noise
        out[name] = jnp.asarray(drawn.astype(out[name].dtype))
    for name, factor in factors.items():
        out[name] = (out[name] * factor).astype(out[name].dtype)
    return out
```

```python
import concourse.bass as bass
from concourse import mybir
from concourse.alu_op_type import AluOpType as ALU
from contextlib import ExitStack

F32 = mybir.dt.float32
U32 = mybir.dt.uint32
ACT = mybir.ActivationFunctionType

P = 128
B = 2048
N = 32
D = 256
C = 16
H1 = 512
H2 = 256
PAIRS = N * (N - 1) // 2
FEAT = PAIRS + C

SPT = P // N
TPQ = 4
TILES = B // SPT
QUADS = TILES // TPQ
GROUP = 512
GROUPS = B // GROUP
QPG = QUADS // GROUPS
TPG = TILES // GROUPS
RING = 8
ROUNDS = QUADS // RING
RPG = QPG // RING
HALF = RPG // 2
KD = D // P
KF = FEAT // P
K1 = H1 // P
K2 = H2 // P
PAIR_AT = [r * (2 * N - r - 1) // 2 for r in range(N)]

T1_BANKS = N // TPQ
A0 = {"t1": 0, "t2": 4, "l1": 6, "l2": 8, "l3": 9, "all": 10}
A1 = {"t1": 0, "t2": 4, "l1": 6, "l2": 8, "all": 9}


def dlrm_tower(nc, table, ids, base, ident, ctx_rows, w1, b1, w2, b2, w3, y):
    stack = ExitStack()
    with stack:
        def sb(name, shape, dt=F32):
            return stack.enter_context(nc.sbuf_tensor(name, shape, dt))

        def ps(name):
            return stack.enter_context(nc.psum_tensor(name, [P, 512], F32))

        def sem(name):
            return stack.enter_context(nc.semaphore(name))

        ids_sb = sb("ids_sb", [P, TILES], mybir.dt.int32)
        base_sb = sb("base_sb", [P, 1])
        ident_sb = sb("ident_sb", [P, P])
        ctx_sb = sb("ctx_sb", [P, GROUPS, SPT, C])
        w1_sb = sb("w1_sb", [P, KF, H1])
        b1_sb = sb("b1_sb", [P, K1])
        w2_sb = sb("w2_sb", [P, K1, H2])
        b2_sb = sb("b2_sb", [P, K2])
        w3_sb = sb("w3_sb", [P, K2])
        row_at = sb("row_at", [P, RING * TPQ], U32)
        rows = sb("rows", [P, RING, TPQ, D])
        rows_t = sb("rows_t", [P, 2, KD, TPQ * P])
        gram = sb("gram", [P, N, TPG])
        feat = sb("feat", [P, SPT, FEAT])
        feat_t = sb("feat_t", [P, KF, GROUP])
        h1 = sb("h1", [P, K1, GROUP])
        h2 = sb("h2", [P, K2, GROUP])
        y_sb = sb("y_sb", [1, B])

        turn_ps = [[ps(f"turn_ps{i}{k}") for k in range(KD)] for i in range(2)]
        gram_ps = [ps(f"gram_ps{i}") for i in range(2)]
        dense_ps = [ps(f"dense_ps{i}") for i in range(2)]

        ids_in = sem("ids_in")
        ident_in = sem("ident_in")
        consts_in = sem("consts_in")
        staged = sem("staged")
        slots_taken = sem("slots_taken")
        landed = [sem(f"landed{s}") for s in range(RING)]
        turned = sem("turned")
        rows_t_dve = sem("rows_t_dve")
        rows_t_act = sem("rows_t_act")
        gram_done = sem("gram_done")
        gram_kept = sem("gram_kept")
        full0, full1 = sem("full0"), sem("full1")
        done0, done1 = sem("done0"), sem("done1")
        stored = sem("stored")

        block = stack.enter_context(nc.Block())

        @block.sync
        def _(sp):
            sp.dma_start(ids_sb[:, :], ids).then_inc(ids_in, 16)
            sp.dma_start(base_sb[:, :], base).then_inc(ids_in, 16)
            sp.dma_start(ident_sb[:, :], ident).then_inc(ident_in, 16)
            sp.dma_start(ctx_sb[:, :, :, :],
                         ctx_rows.rearrange("(g t) (s c) -> t g s c", t=TPG, c=C)).then_inc(consts_in, 16)
            sp.dma_start(w1_sb[:, :, :], w1.rearrange("(k p) n -> p k n", p=P)).then_inc(consts_in, 16)
            sp.dma_start(w2_sb[:, :, :], w2.rearrange("(k p) n -> p k n", p=P)).then_inc(consts_in, 16)
            sp.dma_start(b1_sb[:, :], b1).then_inc(consts_in, 16)
            sp.dma_start(b2_sb[:, :], b2).then_inc(consts_in, 16)
            sp.dma_start(w3_sb[:, :], w3).then_inc(consts_in, 16)
            sp.wait_ge(done0, A0["all"] * GROUPS)
            sp.dma_start(y, y_sb[:, :]).then_inc(stored, 16)
            sp.wait_ge(stored, 16)

        @block.gpsimd
        def _(pool):
            with pool.Fori(0, ROUNDS) as r:
                for s in range(RING):
                    pool.wait_ge(staged, r * RING + (s + 1))
                    pool.sem_inc(slots_taken, 1)
                    for t in range(TPQ):
                        at = s * TPQ + t
                        nc.gpsimd.indirect_dma_start(
                            out=rows[:, s, t, :], out_offset=None, in_=table,
                            in_offset=bass.IndirectOffsetOnAxis(ap=row_at[:, at:at + 1], axis=0),
                        ).then_inc(landed[s], 16)

        @block.tensor
        def _(pe):
            def turn(s, rnd, q):
                pe.wait_ge(landed[s], rnd * (16 * TPQ) + 16 * TPQ)
                if not isinstance(q, int) or q >= 2:
                    pe.wait_ge(rows_t_dve, q - 1)
                    pe.wait_ge(rows_t_act, q - 1)
                for k in range(KD):
                    for t in range(TPQ):
                        last = nc.tensor.transpose(turn_ps[s % 2][k][:, t * P:(t + 1) * P],
                                                   rows[:, s, t, k * P:(k + 1) * P], ident_sb[:, :])
                last.then_inc(turned, 1)

            def gram_of(s, q, first=False):
                pe.wait_ge(rows_t_dve, q + 1)
                pe.wait_ge(rows_t_act, q + 1)
                if not first:
                    pe.wait_ge(gram_kept, q - 1)
                for t in range(TPQ):
                    for k in range(KD):
                        x = rows_t[:, s % 2, k, t * P:(t + 1) * P]
                        last = nc.tensor.matmul(gram_ps[s % 2][:, t * P:(t + 1) * P], x, x,
                                                start=(k == 0), stop=(k == KD - 1))
                last.then_inc(gram_done, 1)

            def pair(s, rnd, first=False):
                q = rnd * RING + s
                if s + 1 < RING:
                    turn(s + 1, rnd, q + 1)
                else:
                    turn(0, rnd + 1, q + 1)
                gram_of(s, q, first)

            def rounds(g, start, end):
                with pe.Fori(start, end) as i:
                    for s in range(RING):
                        pair(s, g * RPG + i)

            def dense_front(g):
                pe.wait_ge(gram_kept, g * QPG + QPG)
                for n in range(T1_BANKS):
                    if n % 2 == 0 and (n or not isinstance(g, int) or g):
                        pe.wait_ge(done0, g * A0["all"] + (A0["t1"] + n // 2))
                    if n % 2 == 1 and (n > 1 or not isinstance(g, int) or g):
                        pe.wait_ge(done1, g * A1["all"] + (A1["t1"] + n // 2))
                    for c in range(TPQ):
                        j = n * TPQ + c
                        if j < N - 1:
                            last = nc.tensor.transpose(dense_ps[n % 2][:, c * P:(c + 1) * P],
                                                       gram[:, j, :], ident_sb[:, :])
                    last.then_inc((full0, full1)[n % 2], 1)
                for k in range(KF):
                    pe.wait_ge(done0, g * A0["all"] + (A0["t2"] + k // 2))
                    pe.wait_ge(done1, g * A1["all"] + (A1["t2"] + k // 2))
                    for c in range(SPT):
                        last = nc.tensor.transpose(dense_ps[k % 2][:, c * P:(c + 1) * P],
                                                   feat[:, c, k * P:(k + 1) * P], ident_sb[:, :])
                    last.then_inc((full0, full1)[k % 2], 1)

            def dense_back(g):
                for m in range(K1):
                    pe.wait_ge(done0, g * A0["all"] + (A0["l1"] + m // 2))
                    pe.wait_ge(done1, g * A1["all"] + (A1["l1"] + m // 2))
                    for k in range(KF):
                        last = nc.tensor.matmul(dense_ps[m % 2][:, :], w1_sb[:, k, m * P:(m + 1) * P],
                                                feat_t[:, k, :], start=(k == 0), stop=(k == KF - 1))
                    last.then_inc((full0, full1)[m % 2], 1)
                pe.wait_ge(done0, g * A0["all"] + A0["l2"])
                pe.wait_ge(done1, g * A1["all"] + A1["l2"])
                for m in range(K2):
                    for k in range(K1):
                        last = nc.tensor.matmul(dense_ps[m % 2][:, :], w2_sb[:, k, m * P:(m + 1) * P],
                                                h1[:, k, :], start=(k == 0), stop=(k == K1 - 1))
                    last.then_inc((full0, full1)[m % 2], 1)
                pe.wait_ge(done0, g * A0["all"] + A0["l3"])
                pe.wait_ge(done1, g * A1["all"] + A1["all"])
                for k in range(K2):
                    last = nc.tensor.matmul(dense_ps[0][0:1, :], w3_sb[:, k:k + 1], h2[:, k, :],
                                            start=(k == 0), stop=(k == K2 - 1))
                last.then_inc(full0, 1)

            pe.wait_ge(ident_in, 16)
            turn(0, 0, 0)
            for s in range(RING):
                pair(s, 0, first=(s < 2))
            rounds(0, 1, RPG)
            pe.wait_ge(consts_in, 16 * 6)
            dense_front(0)
            with pe.Fori(1, GROUPS - 1) as g:
                rounds(g, 0, HALF)
                dense_back(g - 1)
                rounds(g, HALF, RPG)
                dense_front(g)
            rounds(GROUPS - 1, 0, HALF)
            dense_back(GROUPS - 2)
            rounds(GROUPS - 1, HALF, RPG - 1)
            for s in range(RING - 1):
                pair(s, ROUNDS - 1)
            gram_of(RING - 1, QUADS - 1)
            dense_front(GROUPS - 1)
            dense_back(GROUPS - 1)

        @block.vector
        def _(dve):
            def keep_turned(s, q):
                dve.wait_ge(turned, q + 1)
                nc.vector.tensor_copy(rows_t[:, s % 2, 1, :], turn_ps[s % 2][1][:, :]).then_inc(rows_t_dve, 1)

            def stage(s, q):
                nc.vector.tensor_scalar(row_at[:, s * TPQ:(s + 1) * TPQ], ids_sb[:, bass.ds(q * TPQ, TPQ)],
                                        base_sb[:, 0:1], None, ALU.add).then_inc(staged, 1)

            def keep_gram(s, q, tile):
                dve.wait_ge(gram_done, q + 1)
                for c in range(SPT):
                    block_ps = gram_ps[s % 2][c * N:(c + 1) * N, :].rearrange("p (t x) -> p t x", t=TPQ)
                    last = nc.vector.tensor_copy(
                        gram[c * N:(c + 1) * N, :, bass.ds(tile, TPQ)].rearrange("p j t -> p t j"),
                        block_ps[:, :, c * N:(c + 1) * N])
                last.then_inc(gram_kept, 1)

            def rounds(g, start, end):
                with dve.Fori(start, end) as i:
                    for s in range(RING):
                        q = g * QPG + i * RING + s
                        keep_turned(s + 1, q + 1)
                        stage(s, q + RING)
                        keep_gram(s, q, i * (RING * TPQ) + s * TPQ)

            def dense_front(g):
                for n in range(0, T1_BANKS, 2):
                    dve.wait_ge(full0, g * A0["all"] + (A0["t1"] + n // 2 + 1))
                    if n == 0:
                        nc.vector.tensor_copy(feat[:, :, PAIRS:FEAT], ctx_sb[:, g, :, :])
                    for c in range(TPQ):
                        r = n * TPQ + c
                        src = dense_ps[0][:, c * P:(c + 1) * P].rearrange("p (s i) -> p s i", s=SPT)
                        last = nc.vector.tensor_copy(feat[:, :, PAIR_AT[r]:PAIR_AT[r] + N - 1 - r],
                                                     src[:, :, r + 1:N])
                    last.then_inc(done0, 1)
                for k in range(0, KF, 2):
                    dve.wait_ge(full0, g * A0["all"] + (A0["t2"] + k // 2 + 1))
                    nc.vector.tensor_copy(feat_t[:, k, :], dense_ps[0][:, :]).then_inc(done0, 1)

            def dense_back(g):
                for m in range(0, K1, 2):
                    dve.wait_ge(full0, g * A0["all"] + (A0["l1"] + m // 2 + 1))
                    nc.vector.tensor_scalar(h1[:, m, :], dense_ps[0][:, :], b1_sb[:, m:m + 1], 0.0,
                                            ALU.add, ALU.max).then_inc(done0, 1)
                dve.wait_ge(full0, g * A0["all"] + (A0["l2"] + 1))
                nc.vector.tensor_scalar(h2[:, 0, :], dense_ps[0][:, :], b2_sb[:, 0:1], 0.0,
                                        ALU.add, ALU.max).then_inc(done0, 1)
                dve.wait_ge(full0, g * A0["all"] + (A0["l3"] + 1))
                nc.vector.tensor_copy(
                    y_sb[0:1, bass.ds(g * GROUP, GROUP)].rearrange("p (t s) -> p s t", s=SPT),
                    dense_ps[0][0:1, :].rearrange("p (s t) -> p s t", s=SPT)).then_inc(done0, 1)

            dve.wait_ge(ids_in, 32)
            nc.vector.tensor_scalar(row_at[:, :], ids_sb[:, 0:RING * TPQ], base_sb[:, 0:1], None,
                                    ALU.add).then_inc(staged, RING)
            keep_turned(0, 0)
            rounds(0, 0, RPG)
            dve.wait_ge(consts_in, 16 * 6)
            dense_front(0)
            with dve.Fori(1, GROUPS - 1) as g:
                rounds(g, 0, HALF)
                dense_back(g - 1)
                rounds(g, HALF, RPG)
                dense_front(g)
            rounds(GROUPS - 1, 0, HALF)
            dense_back(GROUPS - 2)
            rounds(GROUPS - 1, HALF, RPG - 1)
            for s in range(RING):
                q = (ROUNDS - 1) * RING + s
                if s + 1 < RING:
                    keep_turned(s + 1, q + 1)
                keep_gram(s, q, (RPG - 1) * RING * TPQ + s * TPQ)
            dense_front(GROUPS - 1)
            dense_back(GROUPS - 1)

        @block.scalar
        def _(act):
            def keep_turned(s, q):
                act.wait_ge(turned, q + 1)
                nc.scalar.copy(rows_t[:, s % 2, 0, :], turn_ps[s % 2][0][:, :]).then_inc(rows_t_act, 1)

            def rounds(g, start, end):
                with act.Fori(start, end) as i:
                    for s in range(RING):
                        keep_turned(s + 1, g * QPG + i * RING + (s + 1))

            def dense_front(g):
                for n in range(1, T1_BANKS, 2):
                    act.wait_ge(full1, g * A1["all"] + (A1["t1"] + n // 2 + 1))
                    for c in range(TPQ):
                        r = n * TPQ + c
                        if r < N - 1:
                            src = dense_ps[1][:, c * P:(c + 1) * P].rearrange("p (s i) -> p s i", s=SPT)
                            last = nc.scalar.copy(feat[:, :, PAIR_AT[r]:PAIR_AT[r] + N - 1 - r],
                                                  src[:, :, r + 1:N])
                    last.then_inc(done1, 1)
                for k in range(1, KF, 2):
                    act.wait_ge(full1, g * A1["all"] + (A1["t2"] + k // 2 + 1))
                    nc.scalar.copy(feat_t[:, k, :], dense_ps[1][:, :]).then_inc(done1, 1)

            def dense_back(g):
                for m in range(1, K1, 2):
                    act.wait_ge(full1, g * A1["all"] + (A1["l1"] + m // 2 + 1))
                    nc.scalar.activation(h1[:, m, :], dense_ps[1][:, :], ACT.Relu,
                                         bias=b1_sb[:, m:m + 1]).then_inc(done1, 1)
                act.wait_ge(full1, g * A1["all"] + (A1["l2"] + 1))
                nc.scalar.activation(h2[:, 1, :], dense_ps[1][:, :], ACT.Relu,
                                     bias=b2_sb[:, 1:2]).then_inc(done1, 1)

            keep_turned(0, 0)
            rounds(0, 0, RPG)
            act.wait_ge(consts_in, 16 * 6)
            dense_front(0)
            with act.Fori(1, GROUPS - 1) as g:
                rounds(g, 0, HALF)
                dense_back(g - 1)
                rounds(g, HALF, RPG)
                dense_front(g)
            rounds(GROUPS - 1, 0, HALF)
            dense_back(GROUPS - 2)
            rounds(GROUPS - 1, HALF, RPG - 1)
            for s in range(1, RING):
                keep_turned(s, (ROUNDS - 1) * RING + s)
            dense_front(GROUPS - 1)
            dense_back(GROUPS - 1)


def kernel(dense_ctx, ids, W_top1, b_top1, W_top2, b_top2, W_top3, **tables):
    import numpy as np
    import concourse.bacc as bacc
    from concourse.bass_utils import run_bass_kernel_spmd

    parts = [np.asarray(tables[f"tbl_{f}"]) for f in range(N)]
    first = np.cumsum([0] + [t.shape[0] for t in parts[:-1]])
    arrays = {
        "table": np.concatenate(parts, axis=0),
        "ids": np.ascontiguousarray(np.asarray(ids).reshape(TILES, SPT * N).T),
        "base": np.tile(first, SPT).reshape(P, 1).astype(np.float32),
        "ident": np.eye(P, dtype=np.float32),
        "ctx_rows": np.asarray(dense_ctx).reshape(TILES, SPT * C),
        "w1": np.asarray(W_top1),
        "b1": np.ascontiguousarray(np.asarray(b_top1).reshape(K1, P).T),
        "w2": np.asarray(W_top2),
        "b2": np.ascontiguousarray(np.asarray(b_top2).reshape(K2, P).T),
        "w3": np.ascontiguousarray(np.asarray(W_top3).reshape(K2, P).T),
    }
    nc = bacc.Bacc("TRN2", target_bir_lowering=False, num_devices=1)
    args = [nc.dram_tensor(n, a.shape, mybir.dt.from_np(a.dtype), kind="ExternalInput").ap()
            for n, a in arrays.items()]
    y = nc.dram_tensor("y", (1, B), F32, kind="ExternalOutput").ap()
    dlrm_tower(nc, *args, y)
    result = run_bass_kernel_spmd(nc, [arrays], core_ids=[0])
    return result.results[0]["y"].reshape(B, 1)
```

```python
import concourse.bass as bass
from concourse import mybir
from concourse.alu_op_type import AluOpType as ALU
from contextlib import ExitStack

F32 = mybir.dt.float32
F32R = mybir.dt.float32r
I32 = mybir.dt.int32
U32 = mybir.dt.uint32
ACT = mybir.ActivationFunctionType

P = 128
B = 2048
N = 32
D = 256
C = 16
H1 = 512
H2 = 256
PAIRS = N * (N - 1) // 2
FEAT = PAIRS + C
PAIR_AT = [r * (2 * N - r - 1) // 2 for r in range(N)]
KD = D // P
KF = FEAT // P
K1 = H1 // P
K2 = H2 // P

SELECTED = (26, 28, 30, 31)
NM = len(SELECTED)
NG = N - NM
ORDER = [f for f in range(N) if f not in SELECTED] + list(SELECTED)
VM = 1000
KV = -(-VM // P)
V_LAST = VM - (KV - 1) * P

STEP = 32
FPG = P // STEP
TILES = N // FPG
STEPS = B // STEP
BANKS = 2
TPB = TILES // BANKS
BANK = [TPB, NG // FPG - TPB]
SPB = P // N
BPU = STEP // SPB // BANKS

GROUP = 512
GROUPS = B // GROUP
SPG = GROUP // STEP
BPG = GROUP // SPB
UPG = SPG * BANKS

LOT = 256
LOTS = B // LOT
SPL = LOT // STEP
ROUNDS = STEPS // 2
RPL = SPL // 2
UPL = UPG * LOT // GROUP
HOTS = KV // 2
PIECES = NM * 2

WHOLE, EARLY, LATE = (0, BPG), ((0, 64),), (64, 64)
RUNS = GROUPS + len(EARLY)
MIN_TURN = 72

FILL = {"t1": 0, "t2": 8, "l1": 12, "l2": 16, "l3": 18}
FILLS = (4, 15)

INSIDE = 100


def run_plan(t1, pairs, t2, l1, l2, l3):
    return ([("t1", n, INSIDE + t1) for n in range(8)] + [("pair", n, u) for n, u in enumerate(pairs)]
            + [("t2", n, u) for n, u in enumerate(t2)]
            + [("l1" + "ab"[h % 2], h // 2, u) for h, u in enumerate(l1)]
            + [("l2" + "ab"[h % 2], h // 2, u) for h, u in enumerate(l2)] + [("l3", 0, l3)])


def inside(u):
    return INSIDE + u


DENSE_PLAN = run_plan(0, [0, 1, 1, 2, 3, 4, 5, 6], [4, 5, 6, 7], [8, 10, 12, 14, 16, 18, 20, 22],
                      [24, 26, 28, 30], 31)
FINAL_PLAN = run_plan(0, [0, 0, 1, 1, 2, 2, 3, 3], [4, inside(5), 5, inside(6)],
                      [6, 7, 8, inside(9), 9, 10, inside(11), 11], [12, inside(13), 13, 14], 15)
EARLY_AT = (18,)
EARLY_PLAN = (run_plan(EARLY_AT[0], [18, 18, 19, 19, 20, 20, 21, 21], [21, 22, 22, inside(23)],
                       [23, 23, 24, 24, 25, 25, 26, 26], [27, 27, 28, 28], 29),)
SELECT_AT = [1, 3, 5, 7, 9, 11, 13, 14]
PAIRED = [8 - max(r for r in range(N) if PAIR_AT[r] <= (KF - 1 - n) * P) // 4 for n in range(KF)]


def plan_of(g):
    last = isinstance(g, int) and g == GROUPS - 1
    pieces = []
    if isinstance(g, int) and g == 0:
        pieces += [("split", p, max(0, at - 2), 1, 0) for p, at in enumerate(SELECT_AT)]
    else:
        pieces += [(k, n, u, g - 1, WHOLE) for k, n, u in (FINAL_PLAN if last else DENSE_PLAN)]
    if last:
        for r, (part, steps) in enumerate(zip(EARLY, EARLY_PLAN)):
            pieces += [(k, n, u, g + r, part) for k, n, u in steps]
    for half in range(0 if last else 2):
        lot = g * 2 + half + 1
        for p, at in enumerate(SELECT_AT):
            pieces.append(("sel", p, half * UPL + at, lot, half))
            pieces += [("hot", p * HOTS + c, half * UPL + at - 1, lot, half) for c in range(HOTS)]
    plan = {}
    for kind, n, unit, d, part in sorted(pieces, key=lambda x: x[0] not in ("split", "hot")):
        plan.setdefault(unit, []).append((kind, n, d, part))
    return plan


def late_plan():
    steps = [(k, n) for n in range(8) for k in ("t1", "pair")]
    return steps + [(k, n) for k, n, _ in DENSE_PLAN if k not in ("t1", "pair")]


def turned_blocks(part):
    return max(part[0] + part[1], MIN_TURN)


def owner(fill):
    return 0 if fill < FILL["t2"] and fill % 2 == 0 else 1


def count_of(d, fill):
    return d * FILLS[owner(fill)] + ((fill // 2 if fill < FILL["t2"] else fill - FILL["t2"] + 4) + 1)


def units_until(d, part):
    if part is WHOLE:
        return d * UPG + UPG
    return (GROUPS - 1) * UPG + dict(zip(EARLY, EARLY_AT)).get(part, UPG)


def emptied(wait, done, d, fill):
    wait(done[owner(fill)], count_of(d, fill))


def dlrm_tower(nc, table, ids, base, ident, ids_m, chunk_row, ctx_rows, w1, b1, w2, b2, w3, y):
    stack = ExitStack()
    with stack:
        def sb(name, shape, dt=F32):
            return stack.enter_context(nc.sbuf_tensor(name, shape, dt))

        def ps(name, cols=512):
            return stack.enter_context(nc.psum_tensor(name, [P, cols], F32))

        def sem(name):
            return stack.enter_context(nc.semaphore(name))

        ids_sb = sb("ids_sb", [P, STEPS * TILES], I32)
        base_sb = sb("base_sb", [P, TILES])
        ident_sb = sb("ident_sb", [P, P])
        chunk_row_sb = sb("chunk_row_sb", [P, KV])
        ids_m_sb = sb("ids_m_sb", [P, 2, NM, LOT], I32)
        ctx_sb = sb("ctx_sb", [P, GROUPS, SPB, C])
        w1_sb = sb("w1_sb", [P, KF, H1])
        b1_sb = sb("b1_sb", [P, K1])
        w2_sb = sb("w2_sb", [P, K1, H2])
        b2_sb = sb("b2_sb", [P, K2])
        w3_sb = sb("w3_sb", [P, K2])
        row_at = sb("row_at", [P, 2, TILES], U32)
        rows = sb("rows", [P, 2, TILES, D])
        rows_t = sb("rows_t", [P, 2, 2, KD, STEP * N], F32R)
        tab_hi = sb("tab_hi", [P, NM, KV, D], F32R)
        tab_lo = sb("tab_lo", [P, NM, KV, D], F32R)
        hot = sb("hot", [P, HOTS, LOT], F32R)
        sel_t = sb("sel_t", [P, 2, KD, NM, LOT])
        gram = sb("gram", [P, N, BPG])
        turned_m = sb("turned_m", [P, SPB, N, N])
        flat = turned_m[:, :, :, :].rearrange("p s j i -> p (s j i)")
        h1 = flat[:, 0:K1 * GROUP].rearrange("p (k n) -> p k n", k=K1)
        h2 = flat[:, K1 * GROUP:(K1 + K2) * GROUP].rearrange("p (k n) -> p k n", k=K2)
        feat = sb("feat", [P, SPB, FEAT])
        feat_t = sb("feat_t", [P, KF, GROUP])
        tab_raw = [flat[:, 0:KV * D], flat[:, KV * D:2 * KV * D],
                   feat_t[:, :, :].rearrange("p k n -> p (k n)"),
                   sel_t[:, 0, :, :, :].rearrange("p k f s -> p (k f s)")]
        tab_raw = [t.rearrange("p (c d) -> p c d", c=KV) for t in tab_raw]
        y_sb = sb("y_sb", [1, GROUP])

        turn_ps = [ps(f"turn_ps{k}") for k in range(KD)]
        gram_ps = [ps(f"gram_ps{i}", 1024) for i in range(2)]
        four_ps = [gram_ps[i][:, j * 512:(j + 1) * 512] for i in range(2) for j in range(2)]
        two_ps = [ps("dense_ps"), ps("sel_ps")]
        sel_ps = two_ps[1][:, :].rearrange("p (k s) -> p k s", k=KD)

        ids_in, ids_rest_in, ident_in = sem("ids_in"), sem("ids_rest_in"), sem("ident_in")
        tab_in = [sem(f"tab_in{f}") for f in range(NM)]
        chunk_row_in, consts_in = sem("chunk_row_in"), sem("consts_in")
        ids_m_in = [sem(f"ids_m_in{i}") for i in range(2)]
        staged = sem("staged")
        slots_taken = sem("slots_taken")
        landed = [sem(f"landed{i}") for i in range(2 * BANKS)]
        turned = [sem(f"turned{k}") for k in range(KD)]
        kept_hi = [sem(f"kept_hi{k}") for k in range(KD)]
        kept_lo = [sem(f"kept_lo{k}") for k in range(KD)]
        multiplied = sem("multiplied")
        half_kept = sem("half_kept")
        gram_kept = sem("gram_kept")
        split_hi, split_lo = sem("split_hi"), sem("split_lo")
        hot_done = sem("hot_done")
        sel_done = sem("sel_done")
        sel_kept = sem("sel_kept")
        full = [sem(f"full{i}") for i in range(2)]
        done = [sem(f"done{i}") for i in range(2)]
        paired = sem("paired")
        stored = sem("stored")

        block = stack.enter_context(nc.Block())

        @block.sync
        def _(sp):
            early = 2 * TILES

            def load_ids_m(lot, par=None):
                par = lot % 2 if par is None else par
                sp.dma_start(ids_m_sb[:, par, :, :],
                             ids_m[:, bass.ds(lot * LOT, LOT)].partition_broadcast(P)
                             ).then_inc(ids_m_in[par], 16)

            sp.dma_start(ids_sb[:, 0:early], ids[:, 0:early]).then_inc(ids_in, 16)
            sp.dma_start(ids_sb[:, early:], ids[:, early:]).then_inc(ids_rest_in, 16)
            load_ids_m(1)
            for f in range(NM):
                if f == 0:
                    sp.wait_ge(landed[0], 16 * TPB)
                else:
                    sp.wait_ge(turned[0], BANKS + SELECT_AT[2 * f] - 5)
                first = table.shape[0] - (NM - f) * VM
                sp.dma_start(tab_raw[f][:, 0:KV - 1, :],
                             table[first:first + (KV - 1) * P, :].rearrange("(c p) d -> p c d", p=P)
                             ).then_inc(tab_in[f], 16)
                sp.dma_start(tab_raw[f][0:V_LAST, KV - 1, :], table[first + (KV - 1) * P:first + VM, :]
                             ).then_inc(tab_in[f], 16)
            sp.wait_ge(turned[0], BANKS + SELECT_AT[-1])
            load_ids_m(2)
            sp.dma_start(ctx_sb[:, :, :, :],
                         ctx_rows.rearrange("(g t) (s c) -> t g s c", t=BPG, c=C)).then_inc(consts_in, 16)
            sp.dma_start(w1_sb[:, :, :], w1.rearrange("(k p) n -> p k n", p=P)).then_inc(consts_in, 16)
            sp.dma_start(w2_sb[:, :, :], w2.rearrange("(k p) n -> p k n", p=P)).then_inc(consts_in, 16)
            sp.dma_start(b1_sb[:, :], b1).then_inc(consts_in, 16)
            sp.dma_start(b2_sb[:, :], b2).then_inc(consts_in, 16)
            sp.dma_start(w3_sb[:, :], w3).then_inc(consts_in, 16)
            with sp.Fori(1, GROUPS - 1) as g:
                for lot in range(1, 3):
                    sp.wait_ge(hot_done, g * (2 * PIECES * HOTS) + (lot - 2) * (PIECES * HOTS))
                    load_ids_m(g * 2 + lot, lot % 2)

        @block.gpsimd
        def _(pool):
            def gather(r, bank):
                for par in range(2):
                    for c in range(BANKS):
                        pool.wait_ge(staged, r * (2 * BANKS) + (par * BANKS + c + 1))
                        pool.sem_inc(slots_taken, 1)
                        for t in range(TPB * c, TPB * c + bank[c]):
                            nc.gpsimd.indirect_dma_start(
                                out=rows[:, par, t, :], out_offset=None, in_=table,
                                in_offset=bass.IndirectOffsetOnAxis(ap=row_at[:, par, t:t + 1], axis=0),
                            ).then_inc(landed[par * BANKS + c], 16)

            with pool.Fori(0, RPL) as r:
                gather(r, [TPB] * BANKS)
            with pool.Fori(RPL, ROUNDS - RPL) as r:
                gather(r, BANK)
            with pool.Fori(ROUNDS - RPL, ROUNDS) as r:
                gather(r, [TPB] * BANKS)

        @block.tensor
        def _(pe):
            def turn(par, c, rnd, n):
                tiles = bank_tiles(rnd, c)
                pe.wait_ge(landed[par * BANKS + c], gathers_until(rnd, c) * 16)
                for k in range(KD):
                    if not isinstance(n, int) or n > 0:
                        pe.wait_ge(kept_lo[k], n)
                    for t in range(tiles):
                        last = nc.tensor.transpose(turn_ps[k][:, t * P:(t + 1) * P],
                                                   rows[:, par, TPB * c + t, k * P:(k + 1) * P],
                                                   ident_sb[:, :])
                    last.then_inc(turned[k], 1)

            def multiply(par, c, n):
                if c == 0:
                    for k in range(KD):
                        pe.wait_ge(kept_lo[k], n + BANKS)
                if not isinstance(n, int) or n >= 2:
                    pe.wait_ge(gram_kept, n - 1)
                for b in range(BPU):
                    for k in range(KD):
                        at = (c * BPU + b) * P
                        last = nc.tensor.matmul(
                            gram_ps[c][:, b * 2 * P:(b + 1) * 2 * P].rearrange("p (h x) -> p h x", h=2),
                            rows_t[:, par, 0, k, at:at + P], rows_t[:, par, :, k, at:at + P],
                            start=(k == 0), stop=(k == KD - 1))
                last.then_inc(multiplied, 1)

            def select(piece, lot):
                f, half = divmod(piece, 2)
                pe.wait_ge(hot_done, lot * (PIECES * HOTS) + (piece + 1 - PIECES) * HOTS)
                if isinstance(lot, int) and lot == 1:
                    pe.wait_ge(split_lo, piece + 1)
                if half == 0 and (f or not isinstance(lot, int) or lot > 1):
                    pe.wait_ge(sel_kept, lot * NM + (f - NM))
                for k in range(KD):
                    for c in range(HOTS):
                        v = half * HOTS + c
                        rows_v = V_LAST if v == KV - 1 else P
                        for tab in (tab_hi, tab_lo):
                            last = nc.tensor.matmul(
                                sel_ps[:, k, :], tab[0:rows_v, f, v, k * P:(k + 1) * P],
                                hot[0:rows_v, c, :], start=(v == 0 and k == 0 and tab is tab_hi),
                                stop=(v == KV - 1 and k == KD - 1 and tab is tab_lo))
                last.then_inc(sel_done, 1)

            def dense(kind, n, d, part):
                if kind == "pair":
                    return
                kind, half = kind[:2], kind[2:]
                fill = FILL[kind] + n
                bank = bank_for(four_ps, two_ps, fill, part)
                end = part[0] + part[1]
                cols = SPB * part[1]
                if kind == "t1" and n == 0:
                    pe.wait_ge(gram_kept, units_until(d, part))
                if half != "b":
                    banks = 1 if part is WHOLE else 2
                    if kind == "t1" or part is LATE:
                        if fill >= 4:
                            emptied(pe.wait_ge, done, d, fill - 4)
                    elif fill >= FILL["t2"] + banks:
                        emptied(pe.wait_ge, done, d, fill - banks)
                    elif not isinstance(d, int) or d > 0:
                        pe.wait_ge(done[1], d * FILLS[1])
                if kind == "t1":
                    rows_up = turned_blocks(part)
                    for c in range(4):
                        j = N - 4 * (n + 1) + c
                        last = nc.tensor.transpose(bank[0:rows_up, c * P:(c + 1) * P],
                                                   gram[:, j, 0:rows_up], ident_sb[:, :])
                elif kind == "t2":
                    pe.wait_ge(paired, d * 8 + PAIRED[n])
                    k = KF - 1 - n
                    for c in range(SPB):
                        last = nc.tensor.transpose(bank[:, c * P:c * P + end],
                                                   feat[0:end, c, k * P:(k + 1) * P],
                                                   ident_sb[0:end, 0:end])
                elif kind == "l1":
                    if half != "b":
                        emptied(pe.wait_ge, done, d, FILL["l1"] - 1)
                    for k in halves(KF, half):
                        last = nc.tensor.matmul(bank[:, 0:cols], w1_sb[:, k, n * P:(n + 1) * P],
                                                feat_t[:, k, 0:cols], start=(k == 0), stop=(k == KF - 1))
                elif kind == "l2":
                    if half != "b":
                        emptied(pe.wait_ge, done, d, FILL["l2"] - 1)
                    for k in halves(K1, half):
                        last = nc.tensor.matmul(bank[:, 0:cols], w2_sb[:, k, n * P:(n + 1) * P],
                                                h1[:, k, 0:cols], start=(k == 0), stop=(k == K1 - 1))
                else:
                    emptied(pe.wait_ge, done, d, FILL["l3"] - 1)
                    for k in range(K2):
                        last = nc.tensor.matmul(bank[0:1, 0:cols], w3_sb[:, k:k + 1],
                                                h2[:, k, 0:cols], start=(k == 0), stop=(k == K2 - 1))
                if half != "a":
                    last.then_inc(full[owner(fill)], 1)

            def group(g, plan):
                for u in range(UPG):
                    i, c = divmod(u, BANKS)
                    if not (isinstance(g, int) and g == GROUPS - 1 and i == SPG - 1):
                        turn((i + 1) % 2, c, g * (SPG // 2) + (i + 1) // 2, g * UPG + (u + BANKS))
                    for kind, n, d, part in plan.get(INSIDE + u, ()):
                        dense(kind, n, d, part)
                    for before in range(2):
                        kind, _, d, _ = plan.get(INSIDE + u - before, [("", 0, 0, 0)])[0]
                        if kind == "t1":
                            for fill in range(4 + 2 * c, 6 + 2 * c):
                                emptied(pe.wait_ge, done, d, fill)
                    multiply(i % 2, c, g * UPG + u)
                    for kind, n, d, part in plan.get(u, ()):
                        if kind == "sel":
                            select(n, d)
                        elif kind not in ("hot", "split"):
                            dense(kind, n, d, part)

            pe.wait_ge(ident_in, 16)
            for c in range(BANKS):
                turn(0, c, 0, c)
            group(0, plan_of(0))
            pe.wait_ge(consts_in, 16 * 6)
            with pe.Fori(1, GROUPS - 1) as g:
                group(g, plan_of(g))
            group(GROUPS - 1, plan_of(GROUPS - 1))
            for kind, n in late_plan():
                dense(kind, n, RUNS - 1, LATE)

        @block.vector
        def _(dve):
            def keep_lo(par, c, k, tiles):
                out, src = bank_of(rows_t, turn_ps, par, c, k, 1, tiles)
                hi, _ = bank_of(rows_t, turn_ps, par, c, k, 0, tiles)
                return nc.vector.tensor_tensor(out, src, hi.bitcast(F32), ALU.subtract)

            def keep_lo_selected(par, i):
                out, src = selected_of(rows_t, sel_t, par, i, 1)
                hi, _ = selected_of(rows_t, sel_t, par, i, 0)
                return nc.vector.tensor_tensor(out, src, hi.bitcast(F32), ALU.subtract)

            def keep_turned(par, c, n, i, tiles):
                for k in range(KD):
                    dve.wait_ge(kept_hi[k], n + 1)
                    if k == KD - 1 and tiles < TPB:
                        keep_lo_selected(par, i)
                    keep_lo(par, c, k, tiles).then_inc(kept_lo[k], 1)

            def stage(par, c, step):
                nc.vector.tensor_tensor(row_at[:, par, TPB * c:TPB * (c + 1)],
                                        ids_sb[:, bass.ds(step * TILES + TPB * c, TPB)],
                                        base_sb[:, TPB * c:TPB * (c + 1)], ALU.add).then_inc(staged, 1)

            def keep_gram(c, n, first_block):
                dve.wait_ge(half_kept, n + 1)
                for s in range(SPB):
                    place, _, hi_lo = own_of(gram, gram_ps, c, s, first_block)
                    last = nc.vector.tensor_tensor(place, hi_lo, place, ALU.add)
                last.then_inc(gram_kept, 1)

            def build_hot(chunk, lot, par):
                f, v = divmod(chunk, KV)
                c = v % HOTS
                if chunk == 0:
                    dve.wait_ge(ids_m_in[par], lot * 8 + par * 8)
                if c == 0 and (not isinstance(lot, int) or lot > 1 or chunk):
                    dve.wait_ge(sel_done, lot * PIECES + (chunk // HOTS - PIECES))
                nc.vector.tensor_scalar(hot[:, c, :], ids_m_sb[:, par, f, :],
                                        chunk_row_sb[:, v:v + 1], None, ALU.is_equal).then_inc(hot_done, 1)

            def split(piece):
                dve.wait_ge(split_hi, piece + 1)
                for f, valid, chunks in table_parts(piece):
                    last = nc.vector.tensor_tensor(
                        tab_lo[0:valid, f, chunks, :], tab_raw[f][0:valid, chunks, :],
                        tab_hi[0:valid, f, chunks, :].bitcast(F32), ALU.subtract)
                last.then_inc(split_lo, 1)

            def dense(kind, n, d, part, g):
                blocks = slice(part[0], part[0] + part[1])
                if kind == "pair":
                    for fill in range(max(0, n - 1), n + 1):
                        emptied(dve.wait_ge, done, d, fill)
                    for r in range(N - 4 * (n + 1), N - 4 * n):
                        if r < N - 1:
                            last = nc.vector.tensor_tensor(
                                feat[blocks, :, PAIR_AT[r]:PAIR_AT[r] + N - 1 - r],
                                turned_m[blocks, :, r, r + 1:N], turned_m[blocks, :, r + 1:N, r], ALU.add)
                    last.then_inc(paired, 1)
                    return
                fill = FILL[kind[:2]] + n
                if owner(fill) != 0:
                    return
                dve.wait_ge(full[0], count_of(d, fill))
                if n == 0:
                    nc.vector.tensor_copy(feat[blocks, :, PAIRS:FEAT], ctx_sb[blocks, g, :, :])
                nc.vector.tensor_copy(*columns_of(turned_m, bank_for(four_ps, two_ps, fill, part), n,
                                                  blocks)).then_inc(done[0], 1)

            def group(g, plan):
                last_group = isinstance(g, int) and g == GROUPS - 1
                for u in range(UPG):
                    i, c = divmod(u, BANKS)
                    if not (last_group and i == SPG - 1):
                        keep_turned((i + 1) % 2, c, g * UPG + (u + BANKS), (i + 1) % SPG,
                                    step_tiles(g, i + 1, c))
                    if not (last_group and i + 3 >= SPG):
                        stage((i + 1) % 2, c, g * SPG + (i + 3))
                    for kind, n, d, part in plan.get(INSIDE + u, ()):
                        dense(kind, n, d, part, d if part is WHOLE else GROUPS - 1)
                    keep_gram(c, g * UPG + u, u * BPU)
                    for kind, n, d, part in plan.get(u, ()):
                        if kind == "hot":
                            build_hot(n, d, (part + 1) % 2)
                        elif kind == "split":
                            split(n)
                        elif kind != "sel":
                            dense(kind, n, d, part, d if part is WHOLE else GROUPS - 1)

            dve.wait_ge(ids_in, 32)
            for par in range(2):
                nc.vector.tensor_tensor(row_at[:, par, :], ids_sb[:, par * TILES:(par + 1) * TILES],
                                        base_sb[:, :], ALU.add).then_inc(staged, BANKS)
            dve.wait_ge(ids_rest_in, 16)
            for c in range(BANKS):
                keep_turned(0, c, c, 0, TPB)
                stage(0, c, 2)
            dve.wait_ge(chunk_row_in, 16)
            group(0, plan_of(0))
            dve.wait_ge(consts_in, 16 * 6)
            with dve.Fori(1, GROUPS - 1) as g:
                group(g, plan_of(g))
            group(GROUPS - 1, plan_of(GROUPS - 1))
            for kind, n in late_plan():
                dense(kind, n, RUNS - 1, LATE, GROUPS - 1)

        @block.scalar
        def _(act):
            def keep_turned(par, c, n, i, tiles, lot=None):
                for k in range(KD):
                    act.wait_ge(turned[k], n + 1)
                    if k == KD - 1 and tiles < TPB:
                        if i % SPL == 0:
                            act.wait_ge(sel_kept, lot * NM)
                        nc.scalar.copy(*selected_of(rows_t, sel_t, par, i, 0))
                    nc.scalar.copy(*bank_of(rows_t, turn_ps, par, c, k, 0, tiles)).then_inc(kept_hi[k], 1)

            def keep_half(c, n, first_block):
                act.wait_ge(multiplied, n + 1)
                for s in range(SPB):
                    place, hi_hi, _ = own_of(gram, gram_ps, c, s, first_block)
                    last = nc.scalar.activation(place, hi_hi, ACT.Copy, scale=0.5)
                last.then_inc(half_kept, 1)

            def keep_selected(f, lot, par):
                act.wait_ge(sel_done, lot * PIECES + (2 * (f + 1) - PIECES))
                for k in range(KD):
                    last = nc.scalar.copy(sel_t[:, par, k, f, :], sel_ps[:, k, :])
                last.then_inc(sel_kept, 1)

            def split(piece):
                act.wait_ge(tab_in[piece // 2], 32)
                for f, valid, chunks in table_parts(piece):
                    last = nc.scalar.copy(tab_hi[0:valid, f, chunks, :], tab_raw[f][0:valid, chunks, :])
                last.then_inc(split_hi, 1)

            def dense(kind, n, d, part, g):
                kind, half = kind[:2], kind[2:]
                fill = FILL.get(kind, 0) + n
                if kind == "pa" or half == "a" or owner(fill) != 1:
                    return
                bank = bank_for(four_ps, two_ps, fill, part)
                cols = SPB * part[1]
                blocks = slice(part[0], part[0] + part[1])
                act.wait_ge(full[1], count_of(d, fill))
                if kind == "t1":
                    last = nc.scalar.copy(*columns_of(turned_m, bank, n, blocks))
                elif kind == "t2":
                    last = nc.scalar.copy(*features_of(feat_t, bank, n, blocks, cols))
                elif kind == "l1":
                    last = nc.scalar.activation(h1[:, n, 0:cols], bank[:, 0:cols], ACT.Relu,
                                                bias=b1_sb[:, n:n + 1])
                elif kind == "l2":
                    last = nc.scalar.activation(h2[:, n, 0:cols], bank[:, 0:cols], ACT.Relu,
                                                bias=b2_sb[:, n:n + 1])
                else:
                    if not isinstance(d, int) or d > 0:
                        act.wait_ge(stored, d * 16)
                    last = nc.scalar.copy(y_sb[0:1, 0:cols].rearrange("p (b s) -> p s b", s=SPB),
                                          bank[0:1, 0:cols].rearrange("p (s b) -> p s b", s=SPB))
                last.then_inc(done[1], 1)
                if kind == "l3":
                    emptied(act.wait_ge, done, d, fill)
                    act.dma_start(y[:, bass.ds(g * GROUP + part[0] * SPB, cols)],
                                  y_sb[:, 0:cols]).then_inc(stored, 16)

            def group(g, plan):
                for u in range(UPG):
                    i, c = divmod(u, BANKS)
                    if not (isinstance(g, int) and g == GROUPS - 1 and i == SPG - 1):
                        keep_turned((i + 1) % 2, c, g * UPG + (u + BANKS), (i + 1) % SPG,
                                    step_tiles(g, i + 1, c), g * 2 + (i + 1) // SPL)
                    for kind, n, d, part in plan.get(INSIDE + u, ()):
                        dense(kind, n, d, part, d if part is WHOLE else GROUPS - 1)
                    keep_half(c, g * UPG + u, u * BPU)
                    for kind, n, d, part in plan.get(u, ()):
                        if kind == "sel":
                            if n % 2:
                                keep_selected(n // 2, d, (part + 1) % 2)
                        elif kind == "split":
                            split(n)
                        elif kind != "hot":
                            dense(kind, n, d, part, d if part is WHOLE else GROUPS - 1)

            act.dma_start(base_sb[:, :], base).then_inc(ids_in, 16)
            act.dma_start(ident_sb[:, :], ident).then_inc(ident_in, 16)
            act.dma_start(chunk_row_sb[:, :], chunk_row).then_inc(chunk_row_in, 16)
            for c in range(BANKS):
                keep_turned(0, c, c, 0, TPB)
            group(0, plan_of(0))
            act.wait_ge(consts_in, 16 * 6)
            with act.Fori(1, GROUPS - 1) as g:
                group(g, plan_of(g))
            group(GROUPS - 1, plan_of(GROUPS - 1))
            for kind, n in late_plan():
                dense(kind, n, RUNS - 1, LATE, GROUPS - 1)
            act.wait_ge(stored, 16 * RUNS)


def table_parts(piece):
    f, half = divmod(piece, 2)
    if half == 0:
        return [(f, P, slice(0, HOTS))]
    return [(f, P, slice(HOTS, KV - 1)), (f, V_LAST, slice(KV - 1, KV))]


def halves(count, half):
    return {"": range(count), "a": range(count // 2), "b": range(count // 2, count)}[half]


def bank_tiles(rnd, c):
    return TPB if isinstance(rnd, int) and not RPL <= rnd < ROUNDS - RPL else BANK[c]


def step_tiles(g, i, c):
    return bank_tiles(g * (SPG // 2) + i // 2, c) if isinstance(g, int) else BANK[c]


def gathers_until(rnd, c):
    if isinstance(rnd, int) and rnd < RPL:
        return (rnd + 1) * TPB
    if isinstance(rnd, int) and rnd >= ROUNDS - RPL:
        return (rnd + 1 - (ROUNDS - 2 * RPL)) * TPB + (ROUNDS - 2 * RPL) * BANK[c]
    return rnd * BANK[c] + (BANK[c] + RPL * (TPB - BANK[c]))


def bank_for(four_ps, two_ps, fill, part):
    if fill < FILL["t2"] or part is LATE:
        return four_ps[fill % 4]
    return two_ps[0 if part is WHOLE else fill % 2]


def own_of(gram, gram_ps, c, s, first_block):
    at = slice(s * N, (s + 1) * N)
    own = gram_ps[c][at, :].rearrange("p (b h x) -> p b h x", b=BPU, h=2)
    return (gram[at, :, first_block:first_block + BPU].rearrange("p j b -> p b j"),
            own[:, :, 0, at], own[:, :, 1, at])


def bank_of(rows_t, turn_ps, par, c, k, lo, tiles):
    f0 = c * TPB * FPG
    return (rows_t[:, par, lo, k, :].rearrange("p (s f) -> p f s", f=N)[:, f0:f0 + tiles * FPG, :],
            turn_ps[k][:, 0:tiles * P].rearrange("p (f s) -> p f s", s=STEP))


def selected_of(rows_t, sel_t, par, i, lo):
    lot, step = divmod(i, SPL)
    return (rows_t[:, par, lo, :, :].rearrange("p k (s f) -> p k f s", f=N)[:, :, NG:N, :],
            sel_t[:, lot, :, :, step * STEP:(step + 1) * STEP])


def columns_of(turned_m, bank, n, blocks):
    j0 = N - 4 * (n + 1)
    return (turned_m[blocks, :, j0:j0 + 4, :],
            bank[blocks, :].rearrange("p (j s i) -> p s j i", j=4, s=SPB))


def features_of(feat_t, bank, n, blocks, cols):
    return (feat_t[:, KF - 1 - n, 0:cols].rearrange("p (s b) -> p s b", s=SPB),
            bank[:, :].rearrange("p (s b) -> p s b", s=SPB)[:, :, blocks])


def kernel(dense_ctx, ids, W_top1, b_top1, W_top2, b_top2, W_top3, **tables):
    import numpy as np
    import concourse.bacc as bacc
    from concourse.bass_utils import run_bass_kernel_spmd

    parts = [np.asarray(tables[f"tbl_{f}"]) for f in ORDER]
    first = np.cumsum([0] + [t.shape[0] for t in parts[:N - 1]])
    ids = np.asarray(ids)[:, ORDER]
    pairs = [sorted((ORDER[i], ORDER[j])) for i in range(N) for j in range(i + 1, N)]
    w1_rows = [PAIR_AT[i] + j - i - 1 for i, j in pairs] + list(range(PAIRS, FEAT))
    arrays = {
        "table": np.concatenate(parts, axis=0),
        "ids": np.ascontiguousarray(ids.reshape(STEPS, STEP, TILES, FPG)
                                    .transpose(3, 1, 0, 2).reshape(P, STEPS * TILES)),
        "base": np.repeat(first.reshape(TILES, FPG).T, STEP, axis=0).astype(np.float32),
        "ident": np.eye(P, dtype=np.float32),
        "ids_m": np.ascontiguousarray(ids[:, NG:].T),
        "chunk_row": (np.arange(KV)[None, :] * P + np.arange(P)[:, None]).astype(np.float32),
        "ctx_rows": np.asarray(dense_ctx).reshape(B // SPB, SPB * C),
        "w1": np.asarray(W_top1)[w1_rows],
        "b1": np.ascontiguousarray(np.asarray(b_top1).reshape(K1, P).T),
        "w2": np.asarray(W_top2),
        "b2": np.ascontiguousarray(np.asarray(b_top2).reshape(K2, P).T),
        "w3": np.ascontiguousarray(np.asarray(W_top3).reshape(K2, P).T),
    }
    nc = bacc.Bacc("TRN2", target_bir_lowering=False, num_devices=1)
    args = [nc.dram_tensor(n, a.shape, mybir.dt.from_np(a.dtype), kind="ExternalInput").ap()
            for n, a in arrays.items()]
    y = nc.dram_tensor("y", (1, B), F32, kind="ExternalOutput").ap()
    dlrm_tower(nc, *args, y)
    result = run_bass_kernel_spmd(nc, [arrays], core_ids=[0])
    return result.results[0]["y"].reshape(B, 1)
```

```python
import concourse.bass as bass
from concourse import mybir
from concourse.alu_op_type import AluOpType as ALU
from contextlib import ExitStack

F32 = mybir.dt.float32
F32R = mybir.dt.float32r
I32 = mybir.dt.int32
U32 = mybir.dt.uint32
ACT = mybir.ActivationFunctionType

P = 128
B = 2048
N = 32
D = 256
C = 16
H1 = 512
H2 = 256
PAIRS = N * (N - 1) // 2
FEAT = PAIRS + C
PAIR_AT = [r * (2 * N - r - 1) // 2 for r in range(N)]
KD = D // P
KF = FEAT // P
K1 = H1 // P
K2 = H2 // P

SELECTED = (26, 28, 30, 31)
NM = len(SELECTED)
NG = N - NM
ORDER = [f for f in range(N) if f not in SELECTED] + list(SELECTED)
VM = 1000
KV = -(-VM // P)
V_LAST = VM - (KV - 1) * P

STEP = 32
FPG = P // STEP
TILES = N // FPG
STEPS = B // STEP
BANKS = 2
TPB = TILES // BANKS
BANK = [TPB, NG // FPG - TPB]
SPB = P // N
BPU = STEP // SPB // BANKS

GROUP = 512
GROUPS = B // GROUP
SPG = GROUP // STEP
BPG = GROUP // SPB
UPG = SPG * BANKS

LOT = 256
LOTS = B // LOT
SPL = LOT // STEP
ROUNDS = STEPS // 2
RPL = SPL // 2
UPL = UPG * LOT // GROUP
HOTS = KV // 2
PIECES = NM * 2

WHOLE, EARLY, LATE = (0, BPG), (0, 64), (64, 64)
RUNS = GROUPS + 1
MIN_TURN = 72

FILL = {"t1": 0, "t2": 8, "l1": 12, "l2": 16, "l3": 18}
FILLS = (4, 15)

INSIDE = 100


def run_plan(t1, pairs, t2, l1, l2, l3):
    return ([("t1", n, INSIDE + t1) for n in range(8)] + [("pair", n, u) for n, u in enumerate(pairs)]
            + [("t2", n, u) for n, u in enumerate(t2)]
            + [("l1" + "ab"[h % 2], h // 2, u) for h, u in enumerate(l1)]
            + [("l2" + "ab"[h % 2], h // 2, u) for h, u in enumerate(l2)]
            + [("l3", 0, u) for u in [l3] if u])


def inside(u):
    return INSIDE + u


DENSE_PLAN = run_plan(0, [0, 1, 1, 2, 3, 4, 5, 6], [4, 5, 6, 7], [8, 10, 12, 14, 16, 18, 20, 22],
                      [24, 26, 28, 30], 31)
FINAL_PLAN = run_plan(0, [0, 0, 1, 1, 2, 2, 3, 3], [4, inside(5), 5, inside(6)],
                      [6, 7, 8, inside(9), 9, 10, inside(11), 11], [12, inside(13), 13, 14], 15)
EARLY_AT = 18
EARLY_PLAN = run_plan(EARLY_AT, [18, 18, 18, 19, 19, 19, 20, 20], [20, inside(21), 21, inside(22)],
                      [22, 22, 23, 23, 24, 24, 25, 25], [26, 26, 27, 27], 28)
TAIL = ([(kind, n, LATE) for n in range(8) for kind in ("t1", "pair")]
        + [("t2", n, LATE) for n in range(4)]
        + [("l1", n, LATE) for n in range(4)] + [("l2", n, LATE) for n in range(2)] + [("l3", 0, LATE)])
SELECT_AT = [1, 3, 5, 7, 9, 11, 13, 14]
PAIRED = [8 - max(r for r in range(N) if PAIR_AT[r] <= (KF - 1 - n) * P) // 4 for n in range(KF)]


def plan_of(g):
    last = isinstance(g, int) and g == GROUPS - 1
    pieces = []
    if isinstance(g, int) and g == 0:
        pieces += [("split", p, max(0, at - 2), 1, 0) for p, at in enumerate(SELECT_AT)]
    else:
        pieces += [(k, n, u, g - 1, WHOLE) for k, n, u in (FINAL_PLAN if last else DENSE_PLAN)]
    if last:
        pieces += [(k, n, u, g, EARLY) for k, n, u in EARLY_PLAN]
    for half in range(0 if last else 2):
        lot = g * 2 + half + 1
        for p, at in enumerate(SELECT_AT):
            pieces.append(("sel", p, half * UPL + at, lot, half))
            pieces += [("hot", p * HOTS + c, half * UPL + at - 1, lot, half) for c in range(HOTS)]
    plan = {}
    for kind, n, unit, d, part in sorted(pieces, key=lambda x: x[0] not in ("split", "hot")):
        plan.setdefault(unit, []).append((kind, n, d, part))
    return plan


def turned_blocks(part):
    return max(part[0] + part[1], MIN_TURN)


def owner(fill, part):
    return 0 if fill < FILL["t2"] and fill % 2 == 0 and part is not LATE else 1


def count_of(d, fill, part):
    if part is LATE:
        return fill + 1
    return d * FILLS[owner(fill, part)] + (fill // 2 if fill < FILL["t2"] else fill - FILL["t2"] + 4) + 1


def units_until(d, part):
    if part is WHOLE:
        return d * UPG + UPG
    return (GROUPS - 1) * UPG + (EARLY_AT if part is EARLY else UPG)


def emptied(wait, done, d, fill, part=WHOLE):
    wait(done[owner(fill, part)], count_of(d, fill, part))


def dlrm_tower(nc, table, ids, base, ident, ids_m, chunk_row, ctx_rows, w1, b1, w2, b2, w3, y):
    stack = ExitStack()
    with stack:
        def sb(name, shape, dt=F32):
            return stack.enter_context(nc.sbuf_tensor(name, shape, dt))

        def ps(name, cols=512):
            return stack.enter_context(nc.psum_tensor(name, [P, cols], F32))

        def sem(name):
            return stack.enter_context(nc.semaphore(name))

        ids_sb = sb("ids_sb", [P, STEPS * TILES], I32)
        base_sb = sb("base_sb", [P, TILES])
        ident_sb = sb("ident_sb", [P, P])
        chunk_row_sb = sb("chunk_row_sb", [P, KV])
        ids_m_sb = sb("ids_m_sb", [P, 2, NM, LOT], I32)
        ctx_sb = sb("ctx_sb", [P, GROUPS, SPB, C])
        w1_sb = sb("w1_sb", [P, KF, H1])
        b1_sb = sb("b1_sb", [P, K1])
        w2_sb = sb("w2_sb", [P, K1, H2])
        b2_sb = sb("b2_sb", [P, K2])
        w3_sb = sb("w3_sb", [P, K2])
        row_at = sb("row_at", [P, 2, TILES], U32)
        rows = sb("rows", [P, 2, TILES, D])
        rows_t = sb("rows_t", [P, 2, 2, KD, STEP * N], F32R)
        tab_hi = sb("tab_hi", [P, NM, KV, D], F32R)
        tab_lo = sb("tab_lo", [P, NM, KV, D], F32R)
        hot = sb("hot", [P, HOTS, LOT], F32R)
        sel_t = sb("sel_t", [P, 2, KD, NM, LOT])
        gram = sb("gram", [P, N, BPG])
        turned_m = sb("turned_m", [P, SPB, N, N])
        flat = turned_m[:, :, :, :].rearrange("p s j i -> p (s j i)")
        h1 = flat[:, 0:K1 * GROUP].rearrange("p (k n) -> p k n", k=K1)
        h2 = flat[:, K1 * GROUP:(K1 + K2) * GROUP].rearrange("p (k n) -> p k n", k=K2)
        feat = sb("feat", [P, SPB, FEAT])
        feat_t = sb("feat_t", [P, KF, GROUP])
        spare = sel_t[:, :, :, :, :].rearrange("p l k f s -> p (l k f s)")
        own_layers, used = {}, 0
        for name, part, count in (("h1", EARLY, K1), ("h2", EARLY, K2), ("feat_t", LATE, KF),
                                  ("h1", LATE, K1), ("h2", LATE, K2)):
            size = count * SPB * part[1]
            own_layers[name, part] = spare[:, used:used + size].rearrange("p (k n) -> p k n", k=count)
            used += size
        tab_raw = [flat[:, 0:KV * D], flat[:, KV * D:2 * KV * D],
                   feat_t[:, :, :].rearrange("p k n -> p (k n)"),
                   sel_t[:, 0, :, :, :].rearrange("p k f s -> p (k f s)")]
        tab_raw = [t.rearrange("p (c d) -> p c d", c=KV) for t in tab_raw]
        y_sb = sb("y_sb", [1, GROUP])
        y_late = sb("y_late", [1, SPB * LATE[1]])

        def layer(name, part):
            return own_layers.get((name, part), {"feat_t": feat_t, "h1": h1, "h2": h2}[name])

        turn_ps = [ps(f"turn_ps{k}") for k in range(KD)]
        gram_ps = [ps(f"gram_ps{i}", 1024) for i in range(2)]
        four_ps = [gram_ps[i][:, j * 512:(j + 1) * 512] for i in range(2) for j in range(2)]
        two_ps = [ps("dense_ps"), ps("sel_ps")]
        sel_ps = two_ps[1][:, :].rearrange("p (k s) -> p k s", k=KD)

        ids_in, ids_rest_in, ident_in = sem("ids_in"), sem("ids_rest_in"), sem("ident_in")
        tab_in = [sem(f"tab_in{f}") for f in range(NM)]
        chunk_row_in, consts_in = sem("chunk_row_in"), sem("consts_in")
        ids_m_in = [sem(f"ids_m_in{i}") for i in range(2)]
        staged = sem("staged")
        slots_taken = sem("slots_taken")
        landed = [sem(f"landed{i}") for i in range(2 * BANKS)]
        turned = [sem(f"turned{k}") for k in range(KD)]
        kept_hi = [sem(f"kept_hi{k}") for k in range(KD)]
        kept_lo = [sem(f"kept_lo{k}") for k in range(KD)]
        multiplied = sem("multiplied")
        half_kept = sem("half_kept")
        gram_kept = sem("gram_kept")
        split_hi, split_lo = sem("split_hi"), sem("split_lo")
        hot_done = sem("hot_done")
        sel_done = sem("sel_done")
        sel_kept = sem("sel_kept")
        full = [sem(f"full{i}") for i in range(2)]
        done = [sem(f"done{i}") for i in range(2)]
        paired = sem("paired")
        full_late = [sem(f"full_late{i}") for i in range(2)]
        done_late = [sem(f"done_late{i}") for i in range(2)]
        paired_late = sem("paired_late")
        stored = sem("stored")

        block = stack.enter_context(nc.Block())

        @block.sync
        def _(sp):
            early = 2 * TILES

            def load_ids_m(lot, par):
                sp.dma_start(ids_m_sb[:, par, :, :],
                             ids_m[:, bass.ds(lot * LOT, LOT)].partition_broadcast(P)
                             ).then_inc(ids_m_in[par], 16)

            sp.dma_start(ids_sb[:, 0:early], ids[:, 0:early]).then_inc(ids_in, 16)
            sp.dma_start(ids_sb[:, early:], ids[:, early:]).then_inc(ids_rest_in, 16)
            load_ids_m(1, 1)
            for f in range(NM):
                if f == 0:
                    sp.wait_ge(landed[0], 16 * TPB)
                else:
                    sp.wait_ge(turned[0], BANKS + SELECT_AT[2 * f] - 5)
                first = table.shape[0] - (NM - f) * VM
                sp.dma_start(tab_raw[f][:, 0:KV - 1, :],
                             table[first:first + (KV - 1) * P, :].rearrange("(c p) d -> p c d", p=P)
                             ).then_inc(tab_in[f], 16)
                sp.dma_start(tab_raw[f][0:V_LAST, KV - 1, :], table[first + (KV - 1) * P:first + VM, :]
                             ).then_inc(tab_in[f], 16)
            sp.wait_ge(turned[0], BANKS + SELECT_AT[-1])
            load_ids_m(2, 0)
            sp.dma_start(ctx_sb[:, :, :, :],
                         ctx_rows.rearrange("(g t) (s c) -> t g s c", t=BPG, c=C)).then_inc(consts_in, 16)
            sp.dma_start(w1_sb[:, :, :], w1.rearrange("(k p) n -> p k n", p=P)).then_inc(consts_in, 16)
            sp.dma_start(w2_sb[:, :, :], w2.rearrange("(k p) n -> p k n", p=P)).then_inc(consts_in, 16)
            sp.dma_start(b1_sb[:, :], b1).then_inc(consts_in, 16)
            sp.dma_start(b2_sb[:, :], b2).then_inc(consts_in, 16)
            sp.dma_start(w3_sb[:, :], w3).then_inc(consts_in, 16)
            with sp.Fori(1, GROUPS - 1) as g:
                for lot in range(1, 3):
                    sp.wait_ge(hot_done, g * (2 * PIECES * HOTS) + (lot - 2) * (PIECES * HOTS))
                    load_ids_m(g * 2 + lot, lot % 2)

        @block.gpsimd
        def _(pool):
            def gather(r, bank):
                for par in range(2):
                    for c in range(BANKS):
                        pool.wait_ge(staged, r * (2 * BANKS) + (par * BANKS + c + 1))
                        pool.sem_inc(slots_taken, 1)
                        for t in range(TPB * c, TPB * c + bank[c]):
                            nc.gpsimd.indirect_dma_start(
                                out=rows[:, par, t, :], out_offset=None, in_=table,
                                in_offset=bass.IndirectOffsetOnAxis(ap=row_at[:, par, t:t + 1], axis=0),
                            ).then_inc(landed[par * BANKS + c], 16)

            with pool.Fori(0, RPL) as r:
                gather(r, [TPB] * BANKS)
            with pool.Fori(RPL, ROUNDS - RPL) as r:
                gather(r, BANK)
            with pool.Fori(ROUNDS - RPL, ROUNDS) as r:
                gather(r, [TPB] * BANKS)

        @block.tensor
        def _(pe):
            def turn(par, c, rnd, n):
                tiles = bank_tiles(rnd, c)
                pe.wait_ge(landed[par * BANKS + c], gathers_until(rnd, c) * 16)
                for k in range(KD):
                    if not isinstance(n, int) or n > 0:
                        pe.wait_ge(kept_lo[k], n)
                    for t in range(tiles):
                        last = nc.tensor.transpose(turn_ps[k][:, t * P:(t + 1) * P],
                                                   rows[:, par, TPB * c + t, k * P:(k + 1) * P],
                                                   ident_sb[:, :])
                    last.then_inc(turned[k], 1)

            def multiply(par, c, n):
                if c == 0:
                    for k in range(KD):
                        pe.wait_ge(kept_lo[k], n + BANKS)
                if not isinstance(n, int) or n >= 2:
                    pe.wait_ge(gram_kept, n - 1)
                for b in range(BPU):
                    for k in range(KD):
                        at = (c * BPU + b) * P
                        last = nc.tensor.matmul(
                            gram_ps[c][:, b * 2 * P:(b + 1) * 2 * P].rearrange("p (h x) -> p h x", h=2),
                            rows_t[:, par, 0, k, at:at + P], rows_t[:, par, :, k, at:at + P],
                            start=(k == 0), stop=(k == KD - 1))
                last.then_inc(multiplied, 1)

            def select(piece, lot):
                f, half = divmod(piece, 2)
                pe.wait_ge(hot_done, lot * (PIECES * HOTS) + (piece + 1 - PIECES) * HOTS)
                if isinstance(lot, int) and lot == 1:
                    pe.wait_ge(split_lo, piece + 1)
                if half == 0 and (f or not isinstance(lot, int) or lot > 1):
                    pe.wait_ge(sel_kept, lot * NM + (f - NM))
                for k in range(KD):
                    for c in range(HOTS):
                        v = half * HOTS + c
                        rows_v = V_LAST if v == KV - 1 else P
                        for tab in (tab_hi, tab_lo):
                            last = nc.tensor.matmul(
                                sel_ps[:, k, :], tab[0:rows_v, f, v, k * P:(k + 1) * P],
                                hot[0:rows_v, c, :], start=(v == 0 and k == 0 and tab is tab_hi),
                                stop=(v == KV - 1 and k == KD - 1 and tab is tab_lo))
                last.then_inc(sel_done, 1)

            def dense(kind, n, d, part):
                if kind == "pair":
                    return
                filled, free, pairs = ((full_late, done_late, paired_late) if part is LATE
                                       else (full, done, paired))
                feat_t, h1, h2 = (layer(name, part) for name in ("feat_t", "h1", "h2"))
                kind, half = kind[:2], kind[2:]
                fill = FILL[kind] + n
                bank = bank_for(four_ps, two_ps, fill, part)
                end = part[0] + part[1]
                cols = SPB * part[1]
                if kind == "t1" and n == 0:
                    pe.wait_ge(gram_kept, units_until(d, part))
                if half != "b":
                    banks = 1 if part is WHOLE else 2
                    if kind == "t1" or part is LATE:
                        if fill >= 4:
                            emptied(pe.wait_ge, free, d, fill - 4, part)
                    elif fill >= FILL["t2"] + banks:
                        emptied(pe.wait_ge, free, d, fill - banks, part)
                    elif not isinstance(d, int) or d > 0:
                        pe.wait_ge(free[1], d * FILLS[1])
                if kind == "t1":
                    up_to = turned_blocks(part)
                    for c in range(4):
                        j = N - 4 * (n + 1) + c
                        last = nc.tensor.transpose(bank[0:up_to, c * P:(c + 1) * P],
                                                   gram[:, j, 0:up_to], ident_sb[:, :])
                elif kind == "t2":
                    pe.wait_ge(pairs, d * 8 + PAIRED[n])
                    k = KF - 1 - n
                    for c in range(SPB):
                        last = nc.tensor.transpose(bank[:, c * P:c * P + end],
                                                   feat[0:end, c, k * P:(k + 1) * P],
                                                   ident_sb[0:end, 0:end])
                else:
                    src, weights, chunks = {"l1": (feat_t, w1_sb, KF), "l2": (h1, w2_sb, K1),
                                            "l3": (h2, w3_sb, K2)}[kind]
                    fill_of = [FILL[kind] - 1 - k if kind == "l1" else FILL[kind] - chunks + k
                               for k in range(chunks)]
                    order = sorted(range(chunks), key=lambda k: fill_of[k])
                    rows_out = slice(0, 1 if kind == "l3" else P)
                    for k in halves(order, half):
                        if n == 0:
                            emptied(pe.wait_ge, free, d, fill_of[k], part)
                        w = weights[:, k:k + 1] if kind == "l3" else weights[:, k, n * P:(n + 1) * P]
                        last = nc.tensor.matmul(bank[rows_out, 0:cols], w, src[:, k, 0:cols],
                                                start=(k == order[0]), stop=(k == order[-1]))
                if half != "a":
                    last.then_inc(filled[owner(fill, part)], 1)

            def group(g, plan):
                for u in range(UPG):
                    i, c = divmod(u, BANKS)
                    if not (isinstance(g, int) and g == GROUPS - 1 and i == SPG - 1):
                        turn((i + 1) % 2, c, g * (SPG // 2) + (i + 1) // 2, g * UPG + (u + BANKS))
                    for kind, n, d, part in plan.get(INSIDE + u, ()):
                        dense(kind, n, d, part)
                    for before in range(2):
                        for d in [x[2] for x in plan.get(INSIDE + u - before, ()) if x[:2] == ("t1", 7)]:
                            for fill in range(4 + 2 * c, 6 + 2 * c):
                                emptied(pe.wait_ge, done, d, fill)
                    multiply(i % 2, c, g * UPG + u)
                    for kind, n, d, part in plan.get(u, ()):
                        if kind == "sel":
                            select(n, d)
                        elif kind not in ("hot", "split"):
                            dense(kind, n, d, part)

            pe.wait_ge(ident_in, 16)
            for c in range(BANKS):
                turn(0, c, 0, c)
            group(0, plan_of(0))
            pe.wait_ge(consts_in, 16 * 6)
            with pe.Fori(1, GROUPS - 1) as g:
                group(g, plan_of(g))
            group(GROUPS - 1, plan_of(GROUPS - 1))
            for kind, n, part in TAIL:
                dense(kind, n, GROUPS - 1 if part is EARLY else 0, part)

        @block.vector
        def _(dve):
            def keep_lo(par, c, k, tiles):
                out, src = bank_of(rows_t, turn_ps, par, c, k, 1, tiles)
                hi, _ = bank_of(rows_t, turn_ps, par, c, k, 0, tiles)
                return nc.vector.tensor_tensor(out, src, hi.bitcast(F32), ALU.subtract)

            def keep_lo_selected(par, i):
                out, src = selected_of(rows_t, sel_t, par, i, 1)
                hi, _ = selected_of(rows_t, sel_t, par, i, 0)
                return nc.vector.tensor_tensor(out, src, hi.bitcast(F32), ALU.subtract)

            def keep_turned(par, c, n, i, tiles):
                for k in range(KD):
                    dve.wait_ge(kept_hi[k], n + 1)
                    if k == KD - 1 and tiles < TPB:
                        keep_lo_selected(par, i)
                    keep_lo(par, c, k, tiles).then_inc(kept_lo[k], 1)

            def stage(par, c, step):
                nc.vector.tensor_tensor(row_at[:, par, TPB * c:TPB * (c + 1)],
                                        ids_sb[:, bass.ds(step * TILES + TPB * c, TPB)],
                                        base_sb[:, TPB * c:TPB * (c + 1)], ALU.add).then_inc(staged, 1)

            def keep_gram(c, n, first_block):
                for s in range(SPB):
                    dve.wait_ge(half_kept, n * SPB + (s + 1))
                    place, _, hi_lo = own_of(gram, gram_ps, c, s, first_block)
                    last = nc.vector.tensor_tensor(place, hi_lo, place, ALU.add)
                last.then_inc(gram_kept, 1)

            def build_hot(chunk, lot, par):
                f, v = divmod(chunk, KV)
                c = v % HOTS
                if chunk == 0:
                    dve.wait_ge(ids_m_in[par], lot * 8 + par * 8)
                if c == 0 and (not isinstance(lot, int) or lot > 1 or chunk):
                    dve.wait_ge(sel_done, lot * PIECES + (chunk // HOTS - PIECES))
                nc.vector.tensor_scalar(hot[:, c, :], ids_m_sb[:, par, f, :],
                                        chunk_row_sb[:, v:v + 1], None, ALU.is_equal).then_inc(hot_done, 1)

            def split(piece):
                dve.wait_ge(split_hi, piece + 1)
                for f, valid, chunks in table_parts(piece):
                    last = nc.vector.tensor_tensor(
                        tab_lo[0:valid, f, chunks, :], tab_raw[f][0:valid, chunks, :],
                        tab_hi[0:valid, f, chunks, :].bitcast(F32), ALU.subtract)
                last.then_inc(split_lo, 1)

            def dense(kind, n, d, part, g):
                blocks = slice(part[0], part[0] + part[1])
                filled, free, pairs = ((full_late, done_late, paired_late) if part is LATE
                                       else (full, done, paired))
                if kind == "pair":
                    if n == 0:
                        nc.vector.tensor_copy(feat[blocks, :, PAIRS:FEAT], ctx_sb[blocks, g, :, :])
                    for fill in range(max(0, n - 1), n + 1):
                        emptied(dve.wait_ge, free, d, fill, part)
                    for r in range(N - 4 * (n + 1), N - 4 * n):
                        if r < N - 1:
                            last = nc.vector.tensor_tensor(
                                feat[blocks, :, PAIR_AT[r]:PAIR_AT[r] + N - 1 - r],
                                turned_m[blocks, :, r, r + 1:N], turned_m[blocks, :, r + 1:N, r], ALU.add)
                    last.then_inc(pairs, 1)
                    return
                fill = FILL[kind[:2]] + n
                if owner(fill, part) != 0:
                    return
                dve.wait_ge(filled[0], count_of(d, fill, part))
                nc.vector.tensor_copy(*columns_of(turned_m, bank_for(four_ps, two_ps, fill, part), n,
                                                  blocks)).then_inc(free[0], 1)

            def group(g, plan):
                last_group = isinstance(g, int) and g == GROUPS - 1
                for u in range(UPG):
                    i, c = divmod(u, BANKS)
                    if not (last_group and i == SPG - 1):
                        keep_turned((i + 1) % 2, c, g * UPG + (u + BANKS), (i + 1) % SPG,
                                    step_tiles(g, i + 1, c))
                    if not (last_group and i + 3 >= SPG):
                        stage((i + 1) % 2, c, g * SPG + (i + 3))
                    for kind, n, d, part in plan.get(INSIDE + u, ()):
                        dense(kind, n, d, part, d if part is WHOLE else GROUPS - 1)
                    keep_gram(c, g * UPG + u, u * BPU)
                    for kind, n, d, part in plan.get(u, ()):
                        if kind == "hot":
                            build_hot(n, d, (part + 1) % 2)
                        elif kind == "split":
                            split(n)
                        elif kind != "sel":
                            dense(kind, n, d, part, d if part is WHOLE else GROUPS - 1)

            dve.wait_ge(ids_in, 32)
            for par in range(2):
                nc.vector.tensor_tensor(row_at[:, par, :], ids_sb[:, par * TILES:(par + 1) * TILES],
                                        base_sb[:, :], ALU.add).then_inc(staged, BANKS)
            dve.wait_ge(ids_rest_in, 16)
            for c in range(BANKS):
                keep_turned(0, c, c, 0, TPB)
                stage(0, c, 2)
            dve.wait_ge(chunk_row_in, 16)
            group(0, plan_of(0))
            dve.wait_ge(consts_in, 16 * 6)
            with dve.Fori(1, GROUPS - 1) as g:
                group(g, plan_of(g))
            group(GROUPS - 1, plan_of(GROUPS - 1))
            for kind, n, part in TAIL:
                dense(kind, n, GROUPS - 1 if part is EARLY else 0, part, GROUPS - 1)

        @block.scalar
        def _(act):
            def keep_turned(par, c, n, i, tiles, lot=None):
                for k in range(KD):
                    act.wait_ge(turned[k], n + 1)
                    if k == KD - 1 and tiles < TPB:
                        if i % SPL == 0:
                            act.wait_ge(sel_kept, lot * NM)
                        nc.scalar.copy(*selected_of(rows_t, sel_t, par, i, 0))
                    nc.scalar.copy(*bank_of(rows_t, turn_ps, par, c, k, 0, tiles)).then_inc(kept_hi[k], 1)

            def keep_half(c, n, first_block):
                act.wait_ge(multiplied, n + 1)
                for s in range(SPB):
                    place, hi_hi, _ = own_of(gram, gram_ps, c, s, first_block)
                    nc.scalar.activation(place, hi_hi, ACT.Copy, scale=0.5).then_inc(half_kept, 1)

            def keep_selected(f, lot, par):
                act.wait_ge(sel_done, lot * PIECES + (2 * (f + 1) - PIECES))
                for k in range(KD):
                    last = nc.scalar.copy(sel_t[:, par, k, f, :], sel_ps[:, k, :])
                last.then_inc(sel_kept, 1)

            def split(piece):
                act.wait_ge(tab_in[piece // 2], 32)
                for f, valid, chunks in table_parts(piece):
                    last = nc.scalar.copy(tab_hi[0:valid, f, chunks, :], tab_raw[f][0:valid, chunks, :])
                last.then_inc(split_hi, 1)

            def dense(kind, n, d, part, g):
                kind, half = kind[:2], kind[2:]
                fill = FILL.get(kind, 0) + n
                if kind == "pa" or half == "a" or owner(fill, part) != 1:
                    return
                filled, free = (full_late, done_late) if part is LATE else (full, done)
                feat_t, h1, h2 = (layer(name, part) for name in ("feat_t", "h1", "h2"))
                y_out = y_late if part is LATE else y_sb
                bank = bank_for(four_ps, two_ps, fill, part)
                cols = SPB * part[1]
                blocks = slice(part[0], part[0] + part[1])
                act.wait_ge(filled[1], count_of(d, fill, part))
                if kind == "t1":
                    last = nc.scalar.copy(*columns_of(turned_m, bank, n, blocks))
                elif kind == "t2":
                    last = nc.scalar.copy(*features_of(feat_t, bank, n, blocks, cols))
                elif kind == "l1":
                    last = nc.scalar.activation(h1[:, n, 0:cols], bank[:, 0:cols], ACT.Relu,
                                                bias=b1_sb[:, n:n + 1])
                elif kind == "l2":
                    last = nc.scalar.activation(h2[:, n, 0:cols], bank[:, 0:cols], ACT.Relu,
                                                bias=b2_sb[:, n:n + 1])
                else:
                    if not isinstance(d, int) or d > 0:
                        act.wait_ge(stored, d * 16)
                    last = nc.scalar.copy(y_out[0:1, 0:cols].rearrange("p (b s) -> p s b", s=SPB),
                                          bank[0:1, 0:cols].rearrange("p (s b) -> p s b", s=SPB))
                last.then_inc(free[1], 1)
                if kind == "l3":
                    emptied(act.wait_ge, free, d, fill, part)
                    act.dma_start(y[:, bass.ds(g * GROUP + part[0] * SPB, cols)],
                                  y_out[:, 0:cols]).then_inc(stored, 16)

            def group(g, plan):
                for u in range(UPG):
                    i, c = divmod(u, BANKS)
                    if not (isinstance(g, int) and g == GROUPS - 1 and i == SPG - 1):
                        keep_turned((i + 1) % 2, c, g * UPG + (u + BANKS), (i + 1) % SPG,
                                    step_tiles(g, i + 1, c), g * 2 + (i + 1) // SPL)
                    for kind, n, d, part in plan.get(INSIDE + u, ()):
                        dense(kind, n, d, part, d if part is WHOLE else GROUPS - 1)
                    keep_half(c, g * UPG + u, u * BPU)
                    for kind, n, d, part in plan.get(u, ()):
                        if kind == "sel":
                            if n % 2:
                                keep_selected(n // 2, d, (part + 1) % 2)
                        elif kind == "split":
                            split(n)
                        elif kind != "hot":
                            dense(kind, n, d, part, d if part is WHOLE else GROUPS - 1)

            act.dma_start(base_sb[:, :], base).then_inc(ids_in, 16)
            act.dma_start(ident_sb[:, :], ident).then_inc(ident_in, 16)
            act.dma_start(chunk_row_sb[:, :], chunk_row).then_inc(chunk_row_in, 16)
            for c in range(BANKS):
                keep_turned(0, c, c, 0, TPB)
            group(0, plan_of(0))
            act.wait_ge(consts_in, 16 * 6)
            with act.Fori(1, GROUPS - 1) as g:
                group(g, plan_of(g))
            group(GROUPS - 1, plan_of(GROUPS - 1))
            for kind, n, part in TAIL:
                dense(kind, n, GROUPS - 1 if part is EARLY else 0, part, GROUPS - 1)
            act.wait_ge(stored, 16 * RUNS)


def table_parts(piece):
    f, half = divmod(piece, 2)
    if half == 0:
        return [(f, P, slice(0, HOTS))]
    return [(f, P, slice(HOTS, KV - 1)), (f, V_LAST, slice(KV - 1, KV))]


def halves(chunks, half):
    mid = len(chunks) // 2
    return {"": chunks, "a": chunks[:mid], "b": chunks[mid:]}[half]


def bank_tiles(rnd, c):
    return TPB if isinstance(rnd, int) and not RPL <= rnd < ROUNDS - RPL else BANK[c]


def step_tiles(g, i, c):
    return bank_tiles(g * (SPG // 2) + i // 2, c) if isinstance(g, int) else BANK[c]


def gathers_until(rnd, c):
    if isinstance(rnd, int) and rnd < RPL:
        return (rnd + 1) * TPB
    if isinstance(rnd, int) and rnd >= ROUNDS - RPL:
        return (rnd + 1 - (ROUNDS - 2 * RPL)) * TPB + (ROUNDS - 2 * RPL) * BANK[c]
    return rnd * BANK[c] + (BANK[c] + RPL * (TPB - BANK[c]))


def bank_for(four_ps, two_ps, fill, part):
    if fill < FILL["t2"] or part is LATE:
        return four_ps[fill % 4]
    return two_ps[0 if part is WHOLE else fill % 2]


def own_of(gram, gram_ps, c, s, first_block):
    at = slice(s * N, (s + 1) * N)
    own = gram_ps[c][at, :].rearrange("p (b h x) -> p b h x", b=BPU, h=2)
    return (gram[at, :, first_block:first_block + BPU].rearrange("p j b -> p b j"),
            own[:, :, 0, at], own[:, :, 1, at])


def bank_of(rows_t, turn_ps, par, c, k, lo, tiles):
    f0 = c * TPB * FPG
    return (rows_t[:, par, lo, k, :].rearrange("p (s f) -> p f s", f=N)[:, f0:f0 + tiles * FPG, :],
            turn_ps[k][:, 0:tiles * P].rearrange("p (f s) -> p f s", s=STEP))


def selected_of(rows_t, sel_t, par, i, lo):
    lot, step = divmod(i, SPL)
    return (rows_t[:, par, lo, :, :].rearrange("p k (s f) -> p k f s", f=N)[:, :, NG:N, :],
            sel_t[:, lot, :, :, step * STEP:(step + 1) * STEP])


def columns_of(turned_m, bank, n, blocks):
    j0 = N - 4 * (n + 1)
    return (turned_m[blocks, :, j0:j0 + 4, :],
            bank[blocks, :].rearrange("p (j s i) -> p s j i", j=4, s=SPB))


def features_of(feat_t, bank, n, blocks, cols):
    return (feat_t[:, KF - 1 - n, 0:cols].rearrange("p (s b) -> p s b", s=SPB),
            bank[:, :].rearrange("p (s b) -> p s b", s=SPB)[:, :, blocks])


def kernel(dense_ctx, ids, W_top1, b_top1, W_top2, b_top2, W_top3, **tables):
    import numpy as np
    import concourse.bacc as bacc
    from concourse.bass_utils import run_bass_kernel_spmd

    parts = [np.asarray(tables[f"tbl_{f}"]) for f in ORDER]
    first = np.cumsum([0] + [t.shape[0] for t in parts[:N - 1]])
    ids = np.asarray(ids)[:, ORDER]
    pairs = [sorted((ORDER[i], ORDER[j])) for i in range(N) for j in range(i + 1, N)]
    w1_rows = [PAIR_AT[i] + j - i - 1 for i, j in pairs] + list(range(PAIRS, FEAT))
    arrays = {
        "table": np.concatenate(parts, axis=0),
        "ids": np.ascontiguousarray(ids.reshape(STEPS, STEP, TILES, FPG)
                                    .transpose(3, 1, 0, 2).reshape(P, STEPS * TILES)),
        "base": np.repeat(first.reshape(TILES, FPG).T, STEP, axis=0).astype(np.float32),
        "ident": np.eye(P, dtype=np.float32),
        "ids_m": np.ascontiguousarray(ids[:, NG:].T),
        "chunk_row": (np.arange(KV)[None, :] * P + np.arange(P)[:, None]).astype(np.float32),
        "ctx_rows": np.asarray(dense_ctx).reshape(B // SPB, SPB * C),
        "w1": np.asarray(W_top1)[w1_rows],
        "b1": np.ascontiguousarray(np.asarray(b_top1).reshape(K1, P).T),
        "w2": np.asarray(W_top2),
        "b2": np.ascontiguousarray(np.asarray(b_top2).reshape(K2, P).T),
        "w3": np.ascontiguousarray(np.asarray(W_top3).reshape(K2, P).T),
    }
    nc = bacc.Bacc("TRN2", target_bir_lowering=False, num_devices=1)
    args = [nc.dram_tensor(n, a.shape, mybir.dt.from_np(a.dtype), kind="ExternalInput").ap()
            for n, a in arrays.items()]
    y = nc.dram_tensor("y", (1, B), F32, kind="ExternalOutput").ap()
    dlrm_tower(nc, *args, y)
    result = run_bass_kernel_spmd(nc, [arrays], core_ids=[0])
    return result.results[0]["y"].reshape(B, 1)
```
